# Optimizing a Trainium2 kernel written in Bass

```python
import numpy as np
import jax
import jax.numpy as jnp

def _softmax(x, axis=-1):
    return jax.nn.softmax(x, axis=axis)

def _gelu(x):
    return jax.nn.gelu(x, approximate=True)

def _silu(x):
    return jax.nn.silu(x)

def _sigmoid(x):
    return jax.nn.sigmoid(x)

def _layernorm(x, axis=-1, eps=1e-05):
    m = jnp.mean(x, axis=axis, keepdims=True)
    v = jnp.var(x, axis=axis, keepdims=True)
    return (x - m) / jnp.sqrt(v + eps)

def _scatter_add(tgt, idx, src, axis=0):
    return tgt.at[idx].add(src)

def _segment_sum(src, seg, n):
    return jax.ops.segment_sum(src, seg, n)
kernel_name = 'mk_seq_postln_d1_jaxref_r4_e660eb'

def setup_inputs(seed: int=0):
    np.random.seed(seed)
    _w = jnp.asarray

    def _L0_attn_setup():
        import jax, jax.numpy as jnp
        import numpy as np
        import math
        EPS = 1e-05
        K = 4
        N = 16

        def _causal_depthwise_conv(x, w, b):
            c = x.shape[-1]
            y = jax.lax.conv_general_dilated(x, w, window_strides=(1,), padding=[(K - 1, 0)], dimension_numbers=('NWC', 'WIO', 'NWC'), feature_group_count=c)
            return y + b
        key = jax.random.key(seed)
        b, l, d = (1, 512, 256)
        di = 2 * d
        dt_rank = math.ceil(d / 16)
        ks = jax.random.split(key, 8)
        s = 0.02
        return {'x': jax.random.normal(ks[0], (b, l, d), jnp.float32), 'norm_scale': jnp.ones((d,), jnp.float32), 'w_in': jax.random.normal(ks[1], (d, 4 * d), jnp.float32) * s, 'conv_w': jax.random.normal(ks[2], (K, 1, di), jnp.float32) * 0.2, 'conv_b': jnp.zeros((di,), jnp.float32), 'A_log': jax.random.normal(ks[3], (di, N), jnp.float32) * 0.5, 'D': jax.random.normal(ks[4], (di,), jnp.float32) * 0.1, 'w_xproj': jax.random.normal(ks[5], (di, dt_rank + 2 * N), jnp.float32) * s, 'w_dt': jax.random.normal(ks[6], (dt_rank, di), jnp.float32) * s, 'b_dt': jnp.zeros((di,), jnp.float32), 'w_out': jax.random.normal(ks[7], (di, d), jnp.float32) * s}
    _L0_attn_in = _L0_attn_setup()

    def _L0_ffn_setup():
        import jax, jax.numpy as jnp
        import numpy as np
        D, H, O, E, TOPK = (256, 1024, 256, 8, 2)
        B, S = (4, 256)
        key = jax.random.key(seed)
        ks = jax.random.split(key, 12)
        std = 0.02
        return {'hidden_states': jax.random.normal(ks[0], (B, S, D), dtype=jnp.float32), 'norm_weight': jnp.ones((D,), dtype=jnp.float32), 'router_w': jax.random.normal(ks[1], (E, D), dtype=jnp.float32) * std, 'sw1': jax.random.normal(ks[2], (D, H), dtype=jnp.float32) * (1.0 / np.sqrt(D)), 'sb1': jnp.zeros((H,), dtype=jnp.float32), 'sw2': jax.random.normal(ks[3], (H, O), dtype=jnp.float32) * (1.0 / np.sqrt(H)), 'sb2': jnp.zeros((O,), dtype=jnp.float32), 'ew1': jax.random.normal(ks[4], (E, D, H), dtype=jnp.float32) * (1.0 / np.sqrt(D)), 'eb1': jnp.zeros((E, H), dtype=jnp.float32), 'ew2': jax.random.normal(ks[5], (E, H, O), dtype=jnp.float32) * (1.0 / np.sqrt(H)), 'eb2': jnp.zeros((E, O), dtype=jnp.float32)}
    _L0_ffn_in = _L0_ffn_setup()
    _d = {'L0_attn_x': _L0_attn_in['x'], 'L0_attn_norm_scale': _L0_attn_in['norm_scale'], 'L0_attn_w_in': _L0_attn_in['w_in'], 'L0_attn_conv_w': _L0_attn_in['conv_w'], 'L0_attn_conv_b': _L0_attn_in['conv_b'], 'L0_attn_A_log': _L0_attn_in['A_log'], 'L0_attn_D': _L0_attn_in['D'], 'L0_attn_w_xproj': _L0_attn_in['w_xproj'], 'L0_attn_w_dt': _L0_attn_in['w_dt'], 'L0_attn_b_dt': _L0_attn_in['b_dt'], 'L0_attn_w_out': _L0_attn_in['w_out'], 'L0_ffn_norm_weight': _L0_ffn_in['norm_weight'], 'L0_ffn_router_w': _L0_ffn_in['router_w'], 'L0_ffn_sw1': _L0_ffn_in['sw1'], 'L0_ffn_sb1': _L0_ffn_in['sb1'], 'L0_ffn_sw2': _L0_ffn_in['sw2'], 'L0_ffn_sb2': _L0_ffn_in['sb2'], 'L0_ffn_ew1': _L0_ffn_in['ew1'], 'L0_ffn_eb1': _L0_ffn_in['eb1'], 'L0_ffn_ew2': _L0_ffn_in['ew2'], 'L0_ffn_eb2': _L0_ffn_in['eb2']}
    _x0 = _d['L0_attn_x']
    _d['L0_attn_x'] = jax.random.normal(jax.random.fold_in(jax.random.key(seed), 1), (4, 1024, 256), dtype=_x0.dtype)
    del _x0
    return _d

def reference(L0_attn_x, L0_attn_norm_scale, L0_attn_w_in, L0_attn_conv_w, L0_attn_conv_b, L0_attn_A_log, L0_attn_D, L0_attn_w_xproj, L0_attn_w_dt, L0_attn_b_dt, L0_attn_w_out, L0_ffn_norm_weight, L0_ffn_router_w, L0_ffn_sw1, L0_ffn_sb1, L0_ffn_sw2, L0_ffn_sb2, L0_ffn_ew1, L0_ffn_eb1, L0_ffn_ew2, L0_ffn_eb2):

    def _L0_attn_ref(x, norm_scale, w_in, conv_w, conv_b, A_log, D, w_xproj, w_dt, b_dt, w_out):
        import jax, jax.numpy as jnp
        import numpy as np
        import math
        EPS = 1e-05
        K = 4
        N = 16

        def _causal_depthwise_conv(x, w, b):
            c = x.shape[-1]
            y = jax.lax.conv_general_dilated(x, w, window_strides=(1,), padding=[(K - 1, 0)], dimension_numbers=('NWC', 'WIO', 'NWC'), feature_group_count=c)
            return y + b
        dt_rank = w_dt.shape[0]
        h = x * jax.lax.rsqrt(jnp.mean(x * x, axis=-1, keepdims=True) + EPS) * norm_scale
        h = h @ w_in
        xs, res = jnp.split(h, 2, axis=-1)
        res = jax.nn.silu(res)
        xs = jax.nn.silu(_causal_depthwise_conv(xs, conv_w, conv_b))
        proj = xs @ w_xproj
        delta, B, C = jnp.split(proj, [dt_rank, dt_rank + N], axis=-1)
        delta = jax.nn.softplus(delta @ w_dt + b_dt)
        A = -jnp.exp(A_log)
        deltaA = jnp.exp(delta[..., None] * A)
        deltaBx = (delta * xs)[..., None] * B[:, :, None, :]

        def combine(e_i, e_j):
            a_i, b_i = e_i
            a_j, b_j = e_j
            return (a_i * a_j, a_j * b_i + b_j)
        _, ys = jax.lax.associative_scan(combine, (deltaA, deltaBx), axis=1)
        y = jnp.einsum('blcn,bln->blc', ys, C)
        out = (y + xs * D) * res
        return x + out @ w_out

    def _L0_ffn_ref(hidden_states, norm_weight, router_w, sw1, sb1, sw2, sb2, ew1, eb1, ew2, eb2):
        import jax, jax.numpy as jnp
        import numpy as np
        D, H, O, E, TOPK = (256, 1024, 256, 8, 2)
        B, S = (4, 256)
        b, s, d = hidden_states.shape
        var = jnp.mean(jnp.square(hidden_states), axis=-1, keepdims=True)
        normed = hidden_states * jax.lax.rsqrt(var + 1e-08) * norm_weight
        shared = jnp.maximum(normed @ sw1 + sb1, 0.0) @ sw2 + sb2
        flat = normed.reshape(-1, d)
        T = flat.shape[0]
        probs = jax.nn.sigmoid(flat @ router_w.T)
        scores, idx = jax.lax.top_k(probs, TOPK)
        w = scores / (jnp.sum(scores, axis=-1, keepdims=True) + 1e-06)
        comb = jnp.zeros((T, E), dtype=flat.dtype)
        comb = comb.at[jnp.arange(T)[:, None], idx].add(w)
        h = jnp.maximum(jnp.einsum('td,edh->teh', flat, ew1) + eb1[None, :, :], 0.0)
        eo = jnp.einsum('teh,eho->teo', h, ew2) + eb2[None, :, :]
        routed = jnp.einsum('teo,te->to', eo, comb)
        return shared + routed.reshape(b, s, -1)
    x = L0_attn_x
    x = _layernorm(x + _L0_attn_ref(x, L0_attn_norm_scale, L0_attn_w_in, L0_attn_conv_w, L0_attn_conv_b, L0_attn_A_log, L0_attn_D, L0_attn_w_xproj, L0_attn_w_dt, L0_attn_b_dt, L0_attn_w_out), axis=-1)
    x = _layernorm(x + _L0_ffn_ref(x, L0_ffn_norm_weight, L0_ffn_router_w, L0_ffn_sw1, L0_ffn_sb1, L0_ffn_sw2, L0_ffn_sb2, L0_ffn_ew1, L0_ffn_eb1, L0_ffn_ew2, L0_ffn_eb2), axis=-1)
    return x

_drawn_inputs = setup_inputs


def setup_inputs(seed=0):
    import zlib

    import numpy as np

    out = dict(_drawn_inputs(seed))
    spreads = {'L0_attn_norm_scale': (1.0, 0.6),
     'L0_attn_conv_b': (0.0, 0.8),
     'L0_attn_b_dt': (0.0, 0.8),
     'L0_ffn_norm_weight': (1.0, 0.2),
     'L0_ffn_sb1': (0.0, 0.1),
     'L0_ffn_sb2': (0.0, 0.1),
     'L0_ffn_eb1': (0.0, 0.1),
     'L0_ffn_eb2': (0.0, 0.1)}
    factors = {'L0_attn_w_in': 8.0,
     'L0_attn_conv_w': 8.0,
     'L0_attn_A_log': 8.0,
     'L0_attn_D': 8.0,
     'L0_attn_w_xproj': 8.0,
     'L0_attn_w_dt': 8.0,
     'L0_attn_w_out': 8.0}
    for name, (base, spread) in spreads.items():
        noise = np.random.default_rng([zlib.crc32(name.encode()), seed]).standard_normal(out[name].shape)
        drawn = base * np.exp(spread * noise) if base else spread * noise
        out[name] = jnp.asarray(drawn.astype(out[name].dtype))
    for name, factor in factors.items():
        out[name] = (out[name] * factor).astype(out[name].dtype)
    return out
```

```python
from contextlib import ExitStack

import concourse.bass as bass
from concourse import mybir

ALU = mybir.AluOpType
ACT = mybir.ActivationFunctionType
F32 = mybir.dt.float32
I32 = mybir.dt.int32
U32 = mybir.dt.uint32
AX_X = mybir.AxisListType.X
ds = bass.ds

P = 128
TC = 512
NSUB = TC // P


class Chain:

    def __init__(self, eng, sem):
        self.eng, self.sem, self.before, self.n = eng, sem, 0, 0

    def start(self, before):
        self.before, self.n = before, 0

    def done(self, instruction):
        instruction.then_inc(self.sem, 1)
        self.n += 1
        return self

    def wait(self):
        self.eng.wait_ge(self.sem, self.before + self.n)


def build(nc, x, norm_scale, w_in, conv_w, conv_b, A_log, D_skip, w_xproj, w_dt, b_dt, w_out,
          norm_weight, router_w, sw1, sb1, sw2, sb2, ew1, eb1, ew2, eb2, out):
    NB, L, D = x.shape
    T = NB * L
    NT = T // TC
    HALVES = L // TC
    NSUBS = T // P
    DI = w_in.shape[1] // 2
    CH = DI // P
    N = A_log.shape[1]
    R = w_dt.shape[0]
    K = conv_w.shape[0]
    DC = D // P
    E, H = eb1.shape
    HC = H // P
    O = ew2.shape[2]
    TOPK = 2
    MC = 2 * CH
    assert HALVES == 2 and D == O

    REGION = T + P
    NBLK = (TOPK * T + E * (P - 1)) // P
    NBLK += NBLK % 2
    SPARE = NBLK - TOPK * T // P
    ROWS = E * REGION + SPARE * P

    xt = x.rearrange("b l d -> (b l) d")
    ot = out.rearrange("b l d -> (b l) d")

    bc_dram = nc.dram_tensor("bc_dram", [2, 2 * N, TC], F32).ap()
    rows_dram = nc.dram_tensor("rows_dram", [ROWS, D], F32).ap()
    eo_dram = nc.dram_tensor("eo_dram", [NBLK * P, O], F32).ap()

    vec_parts = [("conv_w", conv_w.rearrange("k o (c p) -> (k o c) p", p=P), K * CH),
                 ("conv_b", conv_b.rearrange("(c p) -> c p", p=P), CH),
                 ("b_dt", b_dt.rearrange("(c p) -> c p", p=P), CH),
                 ("D", D_skip.rearrange("(c p) -> c p", p=P), CH),
                 ("norm_scale", norm_scale.rearrange("(c p) -> c p", p=P), DC),
                 ("norm_weight", norm_weight.rearrange("(c p) -> c p", p=P), DC),
                 ("sb1", sb1.rearrange("(c p) -> c p", p=P), HC),
                 ("eb1", eb1.rearrange("e (c p) -> (e c) p", p=P), E * HC)]
    vec_at, NV = {}, 0
    for name, _, n in vec_parts:
        vec_at[name] = NV
        NV += n
    assert NV <= P

    with ExitStack() as whole:
        def sem(name):
            return whole.enter_context(nc.semaphore(name))

        def alloc(ctx):
            return lambda name, shape, dt=F32: ctx.enter_context(nc.sbuf_tensor(name, shape, dt))

        sb = alloc(whole)
        xall = sb("xall", [P, NSUBS, D])
        ident = sb("ident", [P, P])
        vecs = sb("vecs", [P, NV])
        tri = sb("tri", [P, P])
        ones = sb("ones", [P, P])
        slots = sb("slots", [P, TOPK, NSUBS], U32)
        rows_of = sb("rows_of", [P, TOPK, NSUBS])
        wts = sb("wts", [P, TOPK, NSUBS])
        block_row = sb("block_row", [1, NBLK], I32)
        block_exp = sb("block_exp", [1, NBLK], I32)
        tail_row = sb("tail_row", [1, E], I32)
        psY = whole.enter_context(nc.psum_tensor("psY", [P, CH, TC], F32))
        psA = whole.enter_context(nc.psum_tensor("psA", [P, 2, TC], F32))
        psP = whole.enter_context(nc.psum_tensor("psP", [P, 2, TC], F32))

        def vec(name, i=0):
            a = vec_at[name] + i
            return vecs[:, a:a + 1]


        stage1 = ExitStack()
        sb = alloc(stage1)
        w_in_s = sb("w_in_s", [P, DC, 2 * DI])
        w_xp_s = sb("w_xp_s", [P, CH, R + 2 * N])
        w_dt_s = sb("w_dt_s", [R, DI])
        w_out_s = sb("w_out_s", [P, CH, D])
        convd = sb("convd", [P, K * CH, P])
        skipd = sb("skipd", [P, CH, P])
        A_s = sb("A_s", [P, CH, N])
        carry = sb("carry", [P, CH, N])
        rstd1 = sb("rstd1", [P, NSUBS])
        xr = sb("xr", [P, NSUB, D])
        xnT = sb("xnT", [P, DC, TC])
        xraw = sb("xraw", [P, 2, CH, TC + K - 1])
        xs = sb("xs", [P, CH, TC])
        res = sb("res", [P, 2, CH, TC])
        delta = sb("delta", [P, 2, CH, TC])
        u = sb("u", [P, 2, CH, TC])
        spe = sb("spe", [P, CH, TC])
        spr = sb("spr", [P, CH, TC])
        proj = sb("proj", [R + 2 * N, TC])
        NX = 3
        X = sb("X", [P, NX, CH, TC])
        NBC = 3
        bc = sb("bc", [P, NBC, 2, TC])
        vrows = X[:, 0, 0, 0:P]
        stage1.close()

        stage2 = ExitStack()
        sb = alloc(stage2)
        ew2_s = sb("ew2_s", [P, E, HC, O])
        ew1_s = sb("ew1_s", [P, E, DC, H])
        stage2b = ExitStack()
        sb = alloc(stage2b)
        sw1_s = sb("sw1_s", [P, DC, H])
        sw2_s = sb("sw2_s", [P, HC, O])
        nrm = sb("nrm", [P, NSUB, D])
        nT = sb("nT", [P, DC, TC])
        NH = 2
        hT2 = sb("hT2", [P, NH, TC])
        sb2_s = sb("sb2_s", [P, O])
        junk = sb("junk", [P, D])
        rw = sb("rw", [E, D])
        rwT = sb("rwT", [P, DC, E])
        st6 = sb("st6", [P, NSUB, 6])
        mv = sb("mv", [P, NSUB, 2])
        sc = sb("sc", [P, 6, NSUB])
        prob = sb("prob", [P, NSUB, E])
        cmp = sb("cmp", [P, NSUB, E, E])
        cme = sb("cme", [P, NSUB, E, E])
        lower = sb("lower", [P, E, E])
        rank = sb("rank", [P, NSUB, E])
        top = sb("top", [P, TOPK + 1, NSUB, E])
        pick = sb("pick", [P, 2 * TOPK, NSUB, E])
        picked = sb("picked", [P, 2 * TOPK, NSUB])
        base = sb("base", [P, NSUB + 1, E])
        region = sb("region", [P, E])
        slot = sb("slot", [P, NSUB, E])
        slots_now = sb("slots_now", [P, TOPK, NSUB], U32)
        zero = sb("zero", [P, D])
        nblk = sb("nblk", [P, E])
        nblk_i = sb("nblk_i", [P, E], I32)
        cum = sb("cum", [P, E])
        shift = sb("shift", [P, 3, E])
        shifts = sb("shifts", [P, TOPK * NSUBS])
        row1 = sb("row1", [1, E])
        blk_no = sb("blk_no", [1, NBLK])
        passed = sb("passed", [1, 2, NBLK, E])
        bexp = sb("bexp", [1, 3, NBLK])
        stage2b.close()
        stage3 = ExitStack()
        sb = alloc(stage3)
        xb = sb("xb", [P, 2, D])
        nTb = sb("nTb", [P, 2, DC, P])
        hs = sb("hs", [P, 2, H])
        hT = sb("hT", [P, 2, HC, P])
        eo = sb("eo", [P, 2, O])
        eb2_s = sb("eb2_s", [P, E, O])
        stage3.close()
        stage2.close()
        stage4 = ExitStack()
        sb = alloc(stage4)
        slots4 = sb("slots4", [P, 2, TOPK, NSUB], U32)
        gat = sb("gat", [P, 2, NSUB, TOPK, D])
        st6f = sb("st6f", [P, 2, NSUB, 6])
        mvf = sb("mvf", [P, 2, NSUB, 2])
        scf = sb("scf", [P, 2, 2, NSUB])
        fin = sb("fin", [P, 2, NSUB, D])
        stage4.close()

        s_const = sem("s_const")
        s_w1 = sem("s_w1")
        s_x = sem("s_x")
        s_vecT = sem("s_vecT")
        s_vecs = sem("s_vecs")
        s_setup = sem("s_setup")
        s_ssq = sem("s_ssq")
        xr_ready = sem("xr_ready")
        p_full = sem("p_full")
        p_free = [sem(f"p_free{i}") for i in range(2)]
        xraw_ready = sem("xraw_ready")
        bcw_done = sem("bcw_done")
        bc_here = [sem(f"bc_here{i}") for i in range(NBC)]
        e_ready = sem("e_ready")
        l_ready = sem("l_ready")
        t1_ready = sem("t1_ready")
        sp_link = sem("sp_link")
        delta_ready = sem("delta_ready")
        u_ready = sem("u_ready")
        bx_ready = sem("bx_ready")
        dA_ready = sem("dA_ready")
        scan_done = sem("scan_done")
        carry_done = sem("carry_done")
        hc_ready = sem("hc_ready")
        y_acc = sem("y_acc")
        z_done = sem("z_done")

        s_c2 = sem("s_c2")
        s_passed = sem("s_passed")
        s_w2 = sem("s_w2")
        s_w3 = sem("s_w3")
        rwT_full = sem("rwT_full")
        rwT_ready = sem("rwT_ready")
        v_ready = sem("v_ready")
        sq_ready = sem("sq_ready")
        x2_ready = sem("x2_ready")
        ss_ready = sem("ss_ready")
        nrm_ready = sem("nrm_ready")
        d_link = sem("d_link")
        tr_full = sem("tr_full")
        nT_ready = sem("nT_ready")
        logit_full = sem("logit_full")
        prob_ready = sem("prob_ready")
        sel_ready = sem("sel_ready")
        pos_full = sem("pos_full")
        slots_ready = sem("slots_ready")
        scattered = sem("scattered")
        h_full = sem("h_full")
        relu_done = sem("relu_done")
        o_done = sem("o_done")
        acc_done = sem("acc_done")
        table_ready = sem("table_ready")
        zeroed = sem("zeroed")
        s_eb2 = sem("s_eb2")
        xb_here = [sem(f"xb_here{i}") for i in range(2)]
        T_done = sem("T_done")
        nTb_ready = sem("nTb_ready")
        A_done = sem("A_done")
        hs_ready = sem("hs_ready")
        HT_done = sem("HT_done")
        hb_ready = sem("hb_ready")
        hr_ready = sem("hr_ready")
        B_done = sem("B_done")
        eo_ready = sem("eo_ready")
        eo_out = [sem(f"eo_out{i}") for i in range(2)]
        slots4_ready = sem("slots4_ready")
        gathered = [sem(f"gathered{i}") for i in range(2)]
        v4_ready = sem("v4_ready")
        sq4_ready = sem("sq4_ready")
        f_link = sem("f_link")
        fin_ready = sem("fin_ready")
        out_done = [sem(f"out_done{i}") for i in range(2)]

        block = whole.enter_context(nc.Block())

        P_T, P_I, P_C, P_X, P_D, P_O = 0, DC, DC + MC, DC + MC + CH, DC + MC + CH + 1, DC + MC + 2 * CH + 1
        USES = P_O + 2
        assert USES % 2 == 1

        def bank_of(half, pos):
            return (half * USES + pos) % 2

        def uses_before(b, half, pos):
            return b * USES + (half * USES + pos) // 2

        def tile_count(b, half, per, add=0):
            return b * (2 * per) + (half * per + add)

        def pwait(eng, b, half, pos):
            eng.wait_ge(p_full, tile_count(b, half, USES, pos + 1))
            return psP[:, bank_of(half, pos), :]

        def evacuated(eng, b, half, *positions):
            for pos in positions:
                eng.wait_ge(p_free[bank_of(half, pos)], uses_before(b, half, pos) + 1)

        def settled(eng):
            eng.sem_inc(s_passed, 1)

        def after(eng, sem, count):
            if not isinstance(count, int) or count > 0:
                eng.wait_ge(sem, count)

        def stage1_over(eng):
            for i in range(2):
                eng.wait_ge(p_free[i], NT * USES // 2)

        def stage3_over(eng):
            for i in range(2):
                eng.wait_ge(eo_out[i], 16 * (NBLK // 2))

        LINKS2 = 31
        LINKS4 = 17
        W1_DMAS = len(vec_parts) + 5
        SETUP = 3 + K * CH + CH + 1
        UBC = [len(range(i, N, NBC)) for i in range(NBC)]

        @block.gpsimd
        def _(pool):
            nc.gpsimd.memset(ident[:], 0.0).then_inc(s_const, 1)
            nc.gpsimd.memset(tri[:], 1.0).then_inc(s_const, 1)
            nc.gpsimd.memset(ones[:], 1.0).then_inc(s_const, 1)
            pool.wait_ge(s_const, 3)
            nc.gpsimd.affine_select(out=ident[:], in_=ident[:], compare_op=ALU.not_equal, fill=1.0, base=0,
                                    pattern=[[-1, P]], channel_multiplier=1).then_inc(s_const, 1)
            nc.gpsimd.affine_select(out=tri[:], in_=tri[:], compare_op=ALU.is_gt, fill=0.0, base=0,
                                    pattern=[[1, P]], channel_multiplier=-1).then_inc(s_const, 1)

            def softplus_sum(b, half):
                dl, uu = delta[:, half], u[:, half]
                pool.wait_ge(t1_ready, tile_count(b, half, 1, 1))
                pool.wait_ge(l_ready, tile_count(b, half, 1, 1))
                nc.gpsimd.tensor_tensor(spe[:], spe[:], dl, ALU.subtract).then_inc(sp_link, 1)
                nc.gpsimd.tensor_tensor(spr[:], spr[:], uu, ALU.add).then_inc(sp_link, 1)
                pool.wait_ge(sp_link, tile_count(b, half, 2, 2))
                nc.gpsimd.tensor_tensor(dl, spr[:], spe[:], ALU.add).then_inc(delta_ready, 1)
                pool.wait_ge(delta_ready, tile_count(b, half, 1, 1))
                evacuated(pool, b, half, P_C + CH - 2, P_C + CH - 1)
                nc.gpsimd.tensor_tensor(uu, dl, xs[:], ALU.mult).then_inc(u_ready, 1)

            def input_step(b, half, n):
                if n == 0:
                    pool.wait_ge(u_ready, tile_count(b, half, 1, 1))
                pool.wait_ge(bc_here[n % NBC], tile_count(b, half, 16 * UBC[n % NBC], 16 * (n // NBC + 1)))
                after(pool, y_acc, tile_count(b, half, N, n - NX + 1 if n >= NX else 0))
                nc.gpsimd.tensor_tensor(X[:, n % NX], u[:, half],
                                        bc[:, n % NBC, 0:1, :].broadcast_to([P, CH, TC]),
                                        ALU.mult).then_inc(bx_ready, 1)

            def one_pass(b):
                for half in range(HALVES):
                    softplus_sum(b, half)
                    for n in range(N):
                        input_step(b, half, n)

            one_pass(0)
            with pool.Fori(1, NB) as b:
                one_pass(b)

            stage1_over(pool)
            nc.gpsimd.memset(lower[:], 1.0).then_inc(s_c2, 1)
            nc.gpsimd.memset(zero[:], 0.0).then_inc(s_c2, 1)
            nc.gpsimd.memset(base[:, 0, :], 0.0).then_inc(s_c2, 1)
            nc.gpsimd.iota(region[:], pattern=[[REGION, E]], base=0, channel_multiplier=0,
                           allow_small_or_imprecise_dtypes=True).then_inc(s_c2, 1)
            nc.gpsimd.iota(blk_no[:], pattern=[[1, NBLK]], base=0, channel_multiplier=0,
                           allow_small_or_imprecise_dtypes=True).then_inc(s_c2, 1)
            pool.wait_ge(s_c2, 5)
            nc.gpsimd.affine_select(out=lower[:], in_=lower[:], compare_op=ALU.is_gt, fill=0.0, base=0,
                                    pattern=[[1, E], [-1, E]], channel_multiplier=0).then_inc(s_c2, 1)
            def one_pass(k):
                pool.wait_ge(nrm_ready, k + 1)
                pool.wait_ge(slots_ready, k + 1)
                settled(pool)
                for j in range(TOPK):
                    for s in range(NSUB):
                        nc.gpsimd.indirect_dma_start(
                            out=rows_dram, out_offset=bass.IndirectOffsetOnAxis(ap=slots_now[:, j, s:s + 1], axis=0),
                            in_=nrm[:, s, :], in_offset=None).then_inc(scattered, 16)

            one_pass(0)
            with pool.Fori(1, NT) as k:
                one_pass(k)

            def gather(b, half):
                pool.wait_ge(slots4_ready, b * HALVES + (half + 1))
                settled(pool)
                for s in range(NSUB):
                    for j in range(TOPK):
                        nc.gpsimd.indirect_dma_start(
                            out=gat[:, half, s, j, :], out_offset=None, in_=eo_dram,
                            in_offset=bass.IndirectOffsetOnAxis(ap=slots4[:, half, j, s:s + 1], axis=0)).then_inc(
                            gathered[half], 16)

            stage3_over(pool)
            def one_pass(b):
                for half in range(HALVES):
                    gather(b, half)

            one_pass(0)
            with pool.Fori(1, NB) as b:
                one_pass(b)

        @block.sync
        def _(sp):
            sp.dma_start(xall[:], xt.rearrange("(t p) d -> p t d", p=P)).then_inc(s_x, 16)
            for name, src, n in vec_parts:
                sp.dma_start(vrows[vec_at[name]:vec_at[name] + n, :], src).then_inc(s_w1, 16)
            sp.dma_start(A_s[:], A_log.rearrange("(c p) n -> p c n", p=P)).then_inc(s_w1, 16)
            sp.dma_start(w_in_s[:], w_in.rearrange("(c p) n -> p c n", p=P)).then_inc(s_w1, 16)
            sp.dma_start(w_xp_s[:], w_xproj.rearrange("(c p) n -> p c n", p=P)).then_inc(s_w1, 16)
            sp.dma_start(w_dt_s[:], w_dt).then_inc(s_w1, 16)
            sp.dma_start(w_out_s[:], w_out.rearrange("(c p) n -> p c n", p=P)).then_inc(s_w1, 16)

            def store_bc(b, half):
                evacuated(sp, b, half, P_X)
                sp.dma_start(bc_dram[half], proj[R:R + 2 * N, :]).then_inc(bcw_done, 16)
                sp.wait_ge(bcw_done, tile_count(b, half, 16, 16))

            def load_bc(b, half, n):
                after(sp, hc_ready, tile_count(b, half, N, n - NBC + 1 if n >= NBC else 0))
                src = bc_dram[half].rearrange("(w n) t -> n w t", w=2)[n:n + 1]
                sp.dma_start(bc[:, n % NBC], src.broadcast_to([P, 2, TC])).then_inc(bc_here[n % NBC], 16)

            def one_pass(b):
                for half in range(HALVES):
                    store_bc(b, half)
                    for n in range(N):
                        load_bc(b, half, n)

            one_pass(0)
            with sp.Fori(1, NB) as b:
                one_pass(b)

            stage1_over(sp)
            sp.dma_start(rw[:], router_w).then_inc(s_w2, 16)
            sp.dma_start(sw1_s[:], sw1.rearrange("(c p) n -> p c n", p=P)).then_inc(s_w2, 16)
            sp.dma_start(sw2_s[:], sw2.rearrange("(c p) n -> p c n", p=P)).then_inc(s_w2, 16)
            sp.dma_start(sb2_s[:], sb2.rearrange("(a n) -> a n", a=1).broadcast_to([P, O])).then_inc(s_w2, 16)
            for e in range(E):
                sp.dma_start(ew1_s[:, e], ew1[e].rearrange("(c p) n -> p c n", p=P)).then_inc(s_w3, 16)
                sp.dma_start(ew2_s[:, e], ew2[e].rearrange("(c p) n -> p c n", p=P)).then_inc(s_w3, 16)
            sp.wait_ge(s_c2, 6)
            for i in range(SPARE):
                sp.dma_start(rows_dram[E * REGION + i * P:E * REGION + (i + 1) * P, :], zero[:]).then_inc(zeroed, 16)
            sp.wait_ge(table_ready, 1)
            with sp.Fori(0, E) as e:
                row = sp.value_load(tail_row[0:1, ds(e, 1)], min_val=0, max_val=(E - 1) * REGION + T)
                sp.dma_start(rows_dram[ds(row, P), :], zero[:]).then_inc(zeroed, 16)
            sp.wait_ge(zeroed, 16 * (SPARE + E))
            sp.wait_ge(scattered, 16 * TOPK * NSUBS)
            sp.dma_start(eb2_s[:], eb2.rearrange("(a e) n -> a e n", a=1).broadcast_to([P, E, O])).then_inc(s_eb2, 16)

            def load_block(i, par):
                row = sp.value_load(block_row[0:1, ds(i, 1)], min_val=0, max_val=ROWS - P)
                sp.dma_start(xb[:, par, :], rows_dram[ds(row, P), :]).then_inc(xb_here[par], 16)

            def store_block(i, par):
                sp.wait_ge(eo_ready, i + 1)
                sp.dma_start(eo_dram[ds(i * P, P), :], eo[:, par, :]).then_inc(eo_out[par], 16)

            for i in range(2):
                load_block(i, i)
            def one_pass(t):
                for par in range(2):
                    sp.wait_ge(T_done, t * 2 + (par + 1))
                    load_block(t * 2 + (par + 2), par)
                    store_block(t * 2 + par, par)

            one_pass(0)
            with sp.Fori(1, NBLK // 2 - 1) as t:
                one_pass(t)
            for par in range(2):
                store_block(NBLK - 2 + par, par)

            def one_pass(b):
                for half in range(HALVES):
                    sp.wait_ge(fin_ready, b * HALVES + (half + 1))
                    sp.dma_start(ot.rearrange("(t p) d -> p t d", p=P)[:, ds(b * (HALVES * NSUB) + half * NSUB, NSUB), :],
                                 fin[:, half]).then_inc(out_done[half], 16)

            one_pass(0)
            with sp.Fori(1, NB) as b:
                one_pass(b)
            for half in range(HALVES):
                sp.wait_ge(out_done[half], 16 * NB)

        @block.scalar
        def _(act):
            act.wait_ge(s_x, 16)
            for t in range(NSUBS):
                ins = nc.scalar.activation(spe[:, 0, 0:D], xall[:, t, :], ACT.Square,
                                           accum_out=rstd1[:, t:t + 1]).then_inc(s_ssq, 1)
                act.wait_ge(s_ssq, t + 1)
            act.wait_ge(s_setup, 1)
            nc.scalar.activation(rstd1[:], rstd1[:], ACT.Sqrt).then_inc(s_ssq, 1)
            act.wait_ge(s_w1, W1_DMAS * 16)
            nc.scalar.activation(A_s[:], A_s[:], ACT.Exp).then_inc(s_ssq, 1)
            act.wait_ge(s_vecT, 1)
            nc.scalar.activation(vecs[:], psP[:, 0, 0:NV], ACT.Copy).then_inc(s_vecs, 1)
            act.wait_ge(s_vecs, 1)

            def prep(b, half):
                for d in range(DC):
                    src = pwait(act, b, half, P_T + d)
                    nc.scalar.activation(xnT[:, d, :], src, ACT.Copy, scale=vec("norm_scale", d)).then_inc(
                        p_free[bank_of(half, P_T + d)], 1)
                for m in range(CH):
                    src = pwait(act, b, half, P_I + m)
                    nc.scalar.activation(xraw[:, half, m, K - 1:], src, ACT.Copy).then_inc(
                        p_free[bank_of(half, P_I + m)], 1)
                if half == 1:
                    evacuated(act, b, 1, P_I + CH - 2, P_I + CH - 1)
                    nc.scalar.activation(xraw[:, 1, :, 0:K - 1], xraw[:, 0, :, TC:TC + K - 1],
                                         ACT.Copy).then_inc(xraw_ready, 1)
                for m in range(CH):
                    src = pwait(act, b, half, P_I + CH + m)
                    nc.scalar.activation(res[:, half, m, :], src, ACT.Silu).then_inc(
                        p_free[bank_of(half, P_I + CH + m)], 1)
                after(act, u_ready, tile_count(b, half, 1, 0))
                for c in range(CH):
                    src = pwait(act, b, half, P_C + c)
                    nc.scalar.activation(xs[:, c, :], src, ACT.Silu, bias=vec("conv_b", c)).then_inc(
                        p_free[bank_of(half, P_C + c)], 1)
                src = pwait(act, b, half, P_X)
                nc.scalar.activation(proj[:], src[0:R + 2 * N, :], ACT.Copy).then_inc(
                    p_free[bank_of(half, P_X)], 1)
                for c in range(CH):
                    src = pwait(act, b, half, P_D + c)
                    nc.scalar.activation(spe[:, c, :], src, ACT.Abs, bias=vec("b_dt", c))
                    nc.scalar.activation(spr[:, c, :], src, ACT.Relu, bias=vec("b_dt", c)).then_inc(
                        p_free[bank_of(half, P_D + c)], 1)
                evacuated(act, b, half, P_D + CH - 2, P_D + CH - 1)
                nc.scalar.activation(spe[:], spe[:], ACT.Exp, scale=-1.0).then_inc(e_ready, 1)
                act.wait_ge(e_ready, tile_count(b, half, 1, 1))
                nc.scalar.activation(u[:, half], spe[:], ACT.Ln, bias=1.0).then_inc(l_ready, 1)

            def decay(b, half, n, c):
                if n == 0 and c == 0:
                    act.wait_ge(delta_ready, tile_count(b, half, 1, 1))
                v = n * CH + c
                after(act, scan_done, tile_count(b, half, N * CH, v - 1 if v >= 2 else 0))
                nc.scalar.activation(psA[:, c % 2, :], delta[:, half, c, :], ACT.Exp,
                                     scale=A_s[:, c, n:n + 1]).then_inc(dA_ready, 1)

            def one_pass(b):
                for half in range(HALVES):
                    prep(b, half)
                    for n in range(N):
                        for c in range(CH):
                            decay(b, half, n, c)

            one_pass(0)
            with act.Fori(1, NB) as b:
                one_pass(b)

            stage1_over(act)
            act.wait_ge(rwT_full, 1)
            nc.scalar.activation(rwT[:], psA[:, 0, 0:DC * E].rearrange("p (c e) -> p c e", c=DC),
                                 ACT.Copy).then_inc(rwT_ready, 1)
            def one_pass(k):
                act.wait_ge(v_ready, k * 2 + 1)
                nc.scalar.activation(sc[:, 1, :], sc[:, 0, :], ACT.Sqrt).then_inc(sq_ready, 1)
                act.wait_ge(x2_ready, k + 1)
                for s in range(NSUB):
                    nc.scalar.activation(junk[:], xall[:, k * NSUB + s, :], ACT.Square,
                                         accum_out=sc[:, 3, s:s + 1]).then_inc(ss_ready, 1)
                    act.wait_ge(ss_ready, k * NSUB + (s + 1))
                act.wait_ge(v_ready, k * 2 + 2)
                nc.scalar.activation(sc[:, 5, :], sc[:, 4, :], ACT.Sqrt).then_inc(sq_ready, 1)
                for d in range(DC):
                    act.wait_ge(tr_full, k * DC + (d + 1))
                    nc.scalar.activation(nT[:, d, :], psA[:, d, :], ACT.Copy,
                                         scale=vec("norm_weight", d)).then_inc(nT_ready, 1)
                act.wait_ge(logit_full, k + 1)
                nc.scalar.activation(prob[:], psA[:, 0, 0:NSUB * E].rearrange("p (s e) -> p s e", s=NSUB),
                                     ACT.Exp, scale=-1.0).then_inc(prob_ready, 1)
                for m in range(HC):
                    act.wait_ge(h_full, k * HC + (m + 1))
                    after(act, o_done, k * HC + max(m - 1, 0))
                    nc.scalar.activation(hT2[:, m % NH, :], psP[:, m % 2, :], ACT.Relu,
                                         bias=vec("sb1", m)).then_inc(relu_done, 1)

            one_pass(0)
            with act.Fori(1, NT) as k:
                one_pass(k)

            def scale_rows(i, par):
                act.wait_ge(T_done, i + 1)
                for d in range(DC):
                    ins = nc.scalar.activation(nTb[:, par, d, :], psP[:, 0, d * P:(d + 1) * P], ACT.Copy,
                                               scale=vec("norm_weight", d))
                ins.then_inc(nTb_ready, 1)

            def relu(i, par):
                act.wait_ge(hb_ready, i + 1)
                nc.scalar.activation(hT[:, par], hT[:, par], ACT.Relu).then_inc(hr_ready, 1)

            for i in range(2):
                scale_rows(i, i)
            def one_pass(t):
                for par in range(2):
                    relu(t * 2 + par, par)
                    scale_rows(t * 2 + (par + 2), par)

            one_pass(0)
            with act.Fori(1, NBLK // 2 - 1) as t:
                one_pass(t)
            for par in range(2):
                relu(NBLK - 2 + par, par)

            def one_pass(b):
                for half in range(HALVES):
                    act.wait_ge(v4_ready, b * HALVES + (half + 1))
                    nc.scalar.activation(scf[:, half, 1, :], scf[:, half, 0, :], ACT.Sqrt).then_inc(sq4_ready, 1)

            one_pass(0)
            with act.Fori(1, NB) as b:
                one_pass(b)

        @block.vector
        def _(dve):
            dve.wait_ge(s_ssq, NSUBS)
            nc.vector.tensor_scalar(rstd1[:], rstd1[:], 1.0 / D, 1e-5, ALU.mult, ALU.add).then_inc(s_setup, 1)
            dve.wait_ge(s_ssq, NSUBS + 1)
            nc.vector.reciprocal(rstd1[:], rstd1[:]).then_inc(s_setup, 1)
            dve.wait_ge(s_ssq, NSUBS + 2)
            nc.vector.tensor_scalar(A_s[:], A_s[:], -1.0, None, ALU.mult).then_inc(s_setup, 1)
            dve.wait_ge(s_vecs, 1)
            for i in range(K * CH):
                nc.vector.tensor_scalar(convd[:, i, :], ident[:], vec("conv_w", i), None, ALU.mult).then_inc(s_setup, 1)
            for c in range(CH):
                nc.vector.tensor_scalar(skipd[:, c, :], ident[:], vec("D", c), None, ALU.mult).then_inc(s_setup, 1)
            nc.vector.memset(xraw[:, 0, :, 0:K - 1], 0.0).then_inc(s_setup, 1)
            dve.wait_ge(s_setup, SETUP)

            def norm_rows(b, half, k):
                after(dve, p_full, tile_count(b, half, USES, 0))
                for s in range(NSUB):
                    ins = nc.vector.tensor_scalar(xr[:, s, :], xall[:, k * NSUB + s, :],
                                                  rstd1[:, ds(k * NSUB + s, 1)], None, ALU.mult)
                ins.then_inc(xr_ready, 1)

            def one_plus_e(b, half):
                dve.wait_ge(e_ready, tile_count(b, half, 1, 1))
                nc.vector.tensor_scalar(delta[:, half], spe[:], 1.0, -1.0, ALU.add, ALU.add).then_inc(t1_ready, 1)

            def scan(b, half, n, c):
                dve.wait_ge(dA_ready, tile_count(b, half, N * CH, n * CH + c + 1))
                start = carry[:, c, n:n + 1] if half else 0.0
                nc.vector.tensor_tensor_scan(X[:, n % NX, c, :], psA[:, c % 2, :], X[:, n % NX, c, :], start,
                                             ALU.mult, ALU.add).then_inc(scan_done, 1)

            def keep_state(b, half, n):
                dve.wait_ge(scan_done, tile_count(b, half, N * CH, (n + 1) * CH))
                nc.vector.tensor_copy(carry[:, :, n:n + 1], X[:, n % NX, :, TC - 1:TC]).then_inc(carry_done, 1)

            def output_step(b, half, n):
                dve.wait_ge(scan_done, tile_count(b, half, N * CH, (n + 1) * CH))
                if half == 0:
                    dve.wait_ge(carry_done, b * N + (n + 1))
                nc.vector.tensor_tensor(X[:, n % NX], X[:, n % NX],
                                        bc[:, n % NBC, 1:2, :].broadcast_to([P, CH, TC]),
                                        ALU.mult).then_inc(hc_ready, 1)

            def step(b, half, n):
                dve.wait_ge(bx_ready, tile_count(b, half, N, n + 1))
                if half and n == 0:
                    dve.wait_ge(carry_done, b * N + N)
                for c in range(CH):
                    scan(b, half, n, c)
                    if c == 0 and n and half == 0:
                        keep_state(b, half, n - 1)
                    if c == 1 and n:
                        output_step(b, half, n - 1)

            def gate(b, half):
                dve.wait_ge(y_acc, tile_count(b, half, N, N))
                evacuated(dve, b, half, P_I + MC - 2, P_I + MC - 1)
                nc.vector.tensor_tensor(res[:, half], psY[:], res[:, half], ALU.mult).then_inc(z_done, 1)

            def residual(b, half, k):
                for j in range(2):
                    src = pwait(dve, b, half, P_O + j).rearrange("p (s d) -> p s d", s=2)
                    rows = xall[:, ds(k * NSUB + 2 * j, 2), :]
                    nc.vector.scalar_tensor_tensor(out=rows, in0=rows, scalar=2.0, in1=src,
                                                   op0=ALU.mult, op1=ALU.add).then_inc(
                        p_free[bank_of(half, P_O + j)], 1)

            def one_pass(b):
                for half in range(HALVES):
                    k = b * HALVES + half
                    norm_rows(b, half, k)
                    one_plus_e(b, half)
                    for n in range(N):
                        step(b, half, n)
                    if half == 0:
                        keep_state(b, half, N - 1)
                    output_step(b, half, N - 1)
                    gate(b, half)
                    residual(b, half, k)

            one_pass(0)
            with dve.Fori(1, NB) as b:
                one_pass(b)

            stage1_over(dve)
            dve.wait_ge(s_c2, 6)
            dve.wait_ge(s_w2, 4 * 16)
            link = Chain(dve, d_link)

            def tile2(k):
                rows = xall[:, ds(k * NSUB, NSUB), :]

                def row(s):
                    return xall[:, k * NSUB + s, :]

                settled(dve)
                for s in range(NSUB):
                    ins = nc.vector.bn_stats(out=st6[:, s, :], in_=row(s))
                link.done(ins).wait()
                settled(dve)
                for s in range(NSUB):
                    ins = nc.vector.bn_aggr(out=mv[:, s, :], in_=st6[:, s, :])
                link.done(ins).wait()
                nc.vector.tensor_scalar(sc[:, 0, :], mv[:, :, 1], 1e-5, None, ALU.add).then_inc(v_ready, 1)
                dve.wait_ge(sq_ready, k * 2 + 1)
                link.done(nc.vector.reciprocal(sc[:, 2, :], sc[:, 1, :])).wait()
                for s in range(NSUB):
                    ins = nc.vector.tensor_scalar(row(s), row(s), mv[:, s, 0:1], sc[:, 2, s:s + 1],
                                                  ALU.subtract, ALU.mult)
                ins.then_inc(x2_ready, 1)
                dve.wait_ge(ss_ready, k * NSUB + NSUB)
                nc.vector.tensor_scalar(sc[:, 4, :], sc[:, 3, :], 1.0 / D, 1e-8, ALU.mult, ALU.add).then_inc(v_ready, 1)
                dve.wait_ge(sq_ready, k * 2 + 2)
                link.done(nc.vector.reciprocal(sc[:, 5, :], sc[:, 5, :])).wait()
                after(dve, scattered, k * (16 * TOPK * NSUB))
                dve.wait_ge(x2_ready, k + 1)
                for s in range(NSUB):
                    ins = nc.vector.tensor_scalar(nrm[:, s, :], row(s), sc[:, 5, s:s + 1], None, ALU.mult)
                ins.then_inc(nrm_ready, 1)
                dve.wait_ge(prob_ready, k + 1)
                link.done(nc.vector.tensor_tensor(rows, rows, sb2_s[:].unsqueeze(1).broadcast_to([P, NSUB, O]), ALU.add))
                link.done(nc.vector.tensor_scalar(prob[:], prob[:], 1.0, None, ALU.add)).wait()
                link.done(nc.vector.reciprocal(prob[:], prob[:])).wait()
                p_j = prob[:].unsqueeze(2).broadcast_to([P, NSUB, E, E])
                p_e = prob[:].unsqueeze(3).broadcast_to([P, NSUB, E, E])
                link.done(nc.vector.tensor_tensor(cme[:], p_j, p_e, ALU.is_equal))
                link.done(nc.vector.tensor_tensor(cmp[:], p_j, p_e, ALU.is_gt)).wait()
                link.done(nc.vector.tensor_tensor(cme[:], cme[:], lower[:].unsqueeze(1).broadcast_to([P, NSUB, E, E]),
                                                  ALU.mult)).wait()
                link.done(nc.vector.tensor_tensor(cmp[:], cmp[:], cme[:], ALU.add)).wait()
                link.done(nc.vector.tensor_reduce(rank[:], cmp[:], AX_X, ALU.add)).wait()
                nc.vector.tensor_scalar(top[:, TOPK], rank[:], TOPK - 0.5, None, ALU.is_lt).then_inc(sel_ready, 1)
                for j in range(TOPK):
                    link.done(nc.vector.tensor_scalar(top[:, j], rank[:], float(j), None, ALU.is_equal))
                link.wait()
                for j in range(TOPK):
                    link.done(nc.vector.tensor_tensor(pick[:, j], prob[:], top[:, j], ALU.mult))
                dve.wait_ge(pos_full, k + 1)
                for s in range(NSUB):
                    link.done(nc.vector.tensor_tensor(base[:, s + 1, :], base[:, s, :],
                                                      psA[:, 1, (NSUB + s) * E:(NSUB + s + 1) * E], ALU.add)).wait()
                link.done(nc.vector.tensor_tensor(slot[:], base[:, 0:NSUB, :],
                                                  psA[:, 1, 0:NSUB * E].rearrange("p (s e) -> p s e", s=NSUB),
                                                  ALU.add)).wait()
                link.done(nc.vector.tensor_tensor(slot[:], slot[:], region[:].unsqueeze(1).broadcast_to([P, NSUB, E]),
                                                  ALU.add))
                link.done(nc.vector.tensor_copy(base[:, 0, :], base[:, NSUB, :])).wait()
                for j in range(TOPK):
                    link.done(nc.vector.tensor_tensor(pick[:, TOPK + j], slot[:], top[:, j], ALU.mult))
                link.wait()
                link.done(nc.vector.tensor_reduce(picked[:], pick[:], AX_X, ALU.add)).wait()
                nc.vector.tensor_copy(slots_now[:], picked[:, TOPK:]).then_inc(slots_ready, 1)
                link.done(nc.vector.tensor_copy(rows_of[:, :, ds(k * NSUB, NSUB)], picked[:, TOPK:]))
                link.done(nc.vector.tensor_tensor(sc[:, 0, :], picked[:, 0], picked[:, 1], ALU.add)).wait()
                link.done(nc.vector.tensor_scalar(sc[:, 0, :], sc[:, 0, :], 1e-6, None, ALU.add)).wait()
                link.done(nc.vector.reciprocal(sc[:, 0, :], sc[:, 0, :])).wait()
                link.done(nc.vector.tensor_tensor(wts[:, :, ds(k * NSUB, NSUB)], picked[:, 0:TOPK],
                                                  sc[:, 0:1, :].broadcast_to([P, TOPK, NSUB]), ALU.mult)).wait()
                dve.wait_ge(o_done, k * HC + HC)
                nc.vector.tensor_tensor(rows, rows, psY[:, :, 0:O], ALU.add).then_inc(acc_done, 1)

            def one_pass(k):
                link.start(k * LINKS2)
                tile2(k)
                assert link.n == LINKS2, link.n

            one_pass(0)
            with dve.Fori(1, NT) as k:
                one_pass(k)

            link.start(NT * LINKS2)
            count = base[:, 0, :]
            link.done(nc.vector.tensor_scalar(nblk[:], count, 1.0 / P, (P - 1) / (2.0 * P), ALU.mult, ALU.add)).wait()
            link.done(nc.vector.tensor_copy(nblk_i[:], nblk[:])).wait()
            link.done(nc.vector.tensor_copy(nblk[:], nblk_i[:])).wait()
            link.done(nc.vector.tensor_tensor_scan(cum[:], ones[:, 0:E], nblk[:], 0.0, ALU.mult, ALU.add)).wait()
            i_e = blk_no[:].unsqueeze(2).broadcast_to([1, NBLK, E])
            link.done(nc.vector.tensor_tensor(passed[:, 0], i_e, cum[0:1].unsqueeze(1).broadcast_to([1, NBLK, E]),
                                              ALU.is_ge)).wait()
            link.done(nc.vector.tensor_tensor(passed[:, 1], passed[:, 0],
                                              nblk[0:1].unsqueeze(1).broadcast_to([1, NBLK, E]), ALU.mult)).wait()
            link.done(nc.vector.tensor_reduce(bexp[:, 0:2, :], passed[:], AX_X, ALU.add)).wait()
            link.done(nc.vector.tensor_tensor(bexp[:, 1, :], blk_no[:], bexp[:, 1, :], ALU.subtract)).wait()
            link.done(nc.vector.tensor_scalar(bexp[:, 1, :], bexp[:, 1, :], float(P), None, ALU.mult)).wait()
            link.done(nc.vector.scalar_tensor_tensor(out=bexp[:, 2, :], in0=bexp[:, 0, :], scalar=float(REGION),
                                                     in1=bexp[:, 1, :], op0=ALU.mult, op1=ALU.add))
            link.done(nc.vector.tensor_tensor(row1[:], count[0:1], region[0:1, :], ALU.add)).wait()
            link.done(nc.vector.tensor_tensor(shift[:, 0, :], cum[:], nblk[:], ALU.subtract)).wait()
            link.done(nc.vector.scalar_tensor_tensor(out=shift[:, 1, :], in0=shift[:, 0, :], scalar=float(P),
                                                     in1=region[:], op0=ALU.mult, op1=ALU.subtract)).wait()
            link.done(nc.vector.tensor_copy(shift[:, 2, :], shift[:, 1, :])).wait()
            link.done(nc.vector.tensor_tensor(shift[:, 2, 1:E], shift[:, 1, 1:E], shift[:, 1, 0:E - 1],
                                              ALU.subtract)).wait()
            many = [P, TOPK * NSUBS, E]
            past = nT[:].rearrange("p c t -> p (c t)")[:, 0:TOPK * NSUBS * E].rearrange("p (n e) -> p n e", e=E)
            flat = rows_of[:].rearrange("p j t -> p (j t)")
            link.done(nc.vector.tensor_tensor(past, flat.unsqueeze(2).broadcast_to(many),
                                              region[:].unsqueeze(1).broadcast_to(many), ALU.is_ge)).wait()
            link.done(nc.vector.tensor_tensor(past, past, shift[:, 2:3, :].broadcast_to(many), ALU.mult)).wait()
            link.done(nc.vector.tensor_reduce(shifts[:], past, AX_X, ALU.add)).wait()
            link.done(nc.vector.tensor_tensor(slots[:].rearrange("p j t -> p (j t)"), flat, shifts[:], ALU.add))
            link.done(nc.vector.tensor_copy(block_row[:], bexp[:, 2, :]))
            link.done(nc.vector.tensor_copy(tail_row[:], row1[:])).wait()
            nc.vector.tensor_scalar(block_exp[:], bexp[:, 0, :], float(E - 1), None, ALU.min).then_inc(table_ready, 1)
            dve.wait_ge(table_ready, 1)

            dve.wait_ge(s_eb2, 16)

            def copy_h(i, par):
                dve.wait_ge(A_done, i + 1)
                nc.vector.tensor_copy(hs[:, par, :].rearrange("p (a n) -> p a n", a=2), psA[:]).then_inc(hs_ready, 1)

            def add_b1(i, par, e):
                dve.wait_ge(HT_done, i + 1)
                bias = vecs[:, ds(e * HC + vec_at["eb1"], HC)].unsqueeze(2).broadcast_to([P, HC, P])
                nc.vector.tensor_tensor(hT[:, par], psY[:, 0:2, :].rearrange("p a (c t) -> p (a c) t", t=P), bias,
                                        ALU.add).then_inc(hb_ready, 1)

            def add_b2(i, par, turn, e):
                dve.wait_ge(B_done, i + 1)
                after(dve, eo_out[par], turn * 16)
                nc.vector.tensor_tensor(eo[:, par, :], psP[:, 1, 0:O], eb2_s[:, e, :], ALU.add).then_inc(eo_ready, 1)

            def block3(i, par, turn, last=False):
                e = dve.value_load(block_exp[0:1, ds(i, 1)], min_val=0, max_val=E - 1)
                add_b1(i, par, e)
                if not last:
                    copy_h(i + 1, 1 - par)
                add_b2(i, par, turn, e)

            copy_h(0, 0)
            def one_pass(t):
                for par in range(2):
                    block3(t * 2 + par, par, t)

            one_pass(0)
            with dve.Fori(1, NBLK // 2 - 1) as t:
                one_pass(t)
            for par in range(2):
                block3(NBLK - 2 + par, par, NBLK // 2 - 1, last=(par == 1))

            stage3_over(dve)

            def hand_slots(b, half):
                nc.vector.tensor_copy(slots4[:, half], slots[:, :, ds(b * (HALVES * NSUB) + half * NSUB, NSUB)]).then_inc(
                    slots4_ready, 1)

            def tile4(b, half):
                t0 = b * (HALVES * NSUB) + half * NSUB
                dve.wait_ge(gathered[half], b * (16 * TOPK * NSUB) + 16 * TOPK * NSUB)
                for j in range(TOPK):
                    for s in range(NSUB):
                        link4.done(nc.vector.scalar_tensor_tensor(
                            out=xall[:, t0 + s, :], in0=gat[:, half, s, j, :], scalar=wts[:, j, ds(t0 + s, 1)],
                            in1=xall[:, t0 + s, :], op0=ALU.mult, op1=ALU.add))
                    link4.wait()
                settled(dve)
                for s in range(NSUB):
                    link4.done(nc.vector.bn_stats(out=st6f[:, half, s, :], in_=xall[:, t0 + s, :]))
                link4.wait()
                settled(dve)
                for s in range(NSUB):
                    link4.done(nc.vector.bn_aggr(out=mvf[:, half, s, :], in_=st6f[:, half, s, :]))
                link4.wait()
                nc.vector.tensor_scalar(scf[:, half, 0, :], mvf[:, half, :, 1], 1e-5, None, ALU.add).then_inc(v4_ready, 1)
                dve.wait_ge(sq4_ready, b * HALVES + (half + 1))
                link4.done(nc.vector.reciprocal(scf[:, half, 1, :], scf[:, half, 1, :])).wait()
                after(dve, out_done[half], b * 16)
                for s in range(NSUB):
                    ins = nc.vector.tensor_scalar(fin[:, half, s, :], xall[:, t0 + s, :], mvf[:, half, s, 0:1],
                                                  scf[:, half, 1, s:s + 1], ALU.subtract, ALU.mult)
                ins.then_inc(fin_ready, 1)

            link4 = Chain(dve, f_link)
            for half in range(HALVES):
                hand_slots(0, half)
            def one_pass(b):
                link4.start(b * (HALVES * LINKS4))
                for half in range(HALVES):
                    tile4(b, half)
                    hand_slots(b + 1, half)
                assert link4.n == HALVES * LINKS4, link4.n

            one_pass(0)
            with dve.Fori(1, NB - 1) as b:
                one_pass(b)
            link4.start((NB - 1) * (HALVES * LINKS4))
            for half in range(HALVES):
                tile4(NB - 1, half)

        @block.tensor
        def _(pe):
            pe.wait_ge(s_const, 5)
            pe.wait_ge(s_w1, W1_DMAS * 16)
            nc.tensor.transpose(psP[0:P, 0, 0:NV], vrows[0:NV, :], ident[0:NV, 0:NV]).then_inc(s_vecT, 1)
            pe.wait_ge(s_setup, SETUP)

            def fill(b, half, pos):
                i = bank_of(half, pos)
                after(pe, p_free[i], uses_before(b, half, pos))
                return psP[:, i, :]

            def transposes(b, half):
                pe.wait_ge(xr_ready, tile_count(b, half, 1, 1))
                for d in range(DC):
                    dst = fill(b, half, P_T + d)
                    for s in range(NSUB):
                        ins = nc.tensor.transpose(dst[:, s * P:(s + 1) * P], xr[:, s, d * P:(d + 1) * P], ident[:])
                    ins.then_inc(p_full, 1)

            def in_proj(b, half, m):
                dst = fill(b, half, P_I + m)
                if m == 0:
                    evacuated(pe, b, half, P_T, P_T + 1)
                for d in range(DC):
                    ins = nc.tensor.matmul(dst, w_in_s[:, d, m * P:(m + 1) * P], xnT[:, d, :],
                                           start=(d == 0), stop=(d == DC - 1))
                ins.then_inc(p_full, 1)

            def conv(b, half, c):
                dst = fill(b, half, P_C + c)
                if c == 0:
                    evacuated(pe, b, half, P_I + CH - 2, P_I + CH - 1)
                if half == 1 and c == 0:
                    pe.wait_ge(xraw_ready, b + 1)
                for j in range(K):
                    ins = nc.tensor.matmul(dst, convd[:, j * CH + c, :], xraw[:, half, c, j:j + TC],
                                           start=(j == 0), stop=(j == K - 1))
                ins.then_inc(p_full, 1)

            def x_proj(b, half):
                dst = fill(b, half, P_X)
                evacuated(pe, b, half, P_C + CH - 2, P_C + CH - 1)
                for c in range(CH):
                    ins = nc.tensor.matmul(dst[0:R + 2 * N, :], w_xp_s[:, c, :], xs[:, c, :],
                                           start=(c == 0), stop=(c == CH - 1))
                ins.then_inc(p_full, 1)

            def dt_proj(b, half, c):
                dst = fill(b, half, P_D + c)
                if c == 0:
                    evacuated(pe, b, half, P_X)
                nc.tensor.matmul(dst, w_dt_s[:, c * P:(c + 1) * P], proj[0:R, :],
                                 start=True, stop=True).then_inc(p_full, 1)

            def skip(b, half):
                after(pe, z_done, tile_count(b, half, 1, 0))
                for c in range(CH):
                    nc.tensor.matmul(psY[:, c, :], skipd[:, c, :], xs[:, c, :], start=True, stop=False)

            def add_state(b, half, n):
                pe.wait_ge(hc_ready, tile_count(b, half, N, n + 1))
                for c in range(CH):
                    ins = nc.tensor.matmul(psY[:, c, :], ident[:], X[:, n % NX, c, :],
                                           start=False, stop=(n == N - 1))
                ins.then_inc(y_acc, 1)

            def out_proj(b, half):
                pe.wait_ge(z_done, tile_count(b, half, 1, 1))
                for j in range(2):
                    dst = fill(b, half, P_O + j)
                    for i in range(2):
                        s = 2 * j + i
                        for c in range(CH):
                            ins = nc.tensor.matmul(dst[:, i * D:(i + 1) * D], res[:, half, c, s * P:(s + 1) * P],
                                                   w_out_s[:, c, :], start=(c == 0), stop=(c == CH - 1))
                    ins.then_inc(p_full, 1)

            def one_pass(b):
                for half in range(HALVES):
                    transposes(b, half)
                    for m in range(MC):
                        in_proj(b, half, m)
                    for c in range(CH):
                        conv(b, half, c)
                    x_proj(b, half)
                    for c in range(CH):
                        dt_proj(b, half, c)
                    skip(b, half)
                    for n in range(N):
                        add_state(b, half, n)
                    out_proj(b, half)

            one_pass(0)
            with pe.Fori(1, NB) as b:
                one_pass(b)

            stage1_over(pe)
            pe.wait_ge(s_w2, 4 * 16)
            for d in range(DC):
                ins = nc.tensor.transpose(psA[:, 0, d * E:(d + 1) * E], rw[:, d * P:(d + 1) * P], ident[0:E, 0:E])
            ins.then_inc(rwT_full, 1)
            pe.wait_ge(rwT_ready, 1)

            def up(k, m):
                after(pe, relu_done, k * HC + max(m - 1, 0))
                for d in range(DC):
                    ins = nc.tensor.matmul(psP[:, m % 2, :], sw1_s[:, d, m * P:(m + 1) * P], nT[:, d, :],
                                           start=(d == 0), stop=(d == DC - 1))
                ins.then_inc(h_full, 1)

            def down(k, m):
                pe.wait_ge(relu_done, k * HC + (m + 1))
                if m == 0:
                    after(pe, acc_done, k)
                for s in range(NSUB):
                    ins = nc.tensor.matmul(psY[:, s, 0:O], hT2[:, m % NH, s * P:(s + 1) * P], sw2_s[:, m, :],
                                           start=(m == 0), stop=(m == HC - 1))
                ins.then_inc(o_done, 1)

            def positions(k):
                pe.wait_ge(sel_ready, k + 1)
                sel = top[:, TOPK].rearrange("p s e -> p (s e)")
                nc.tensor.matmul(psA[:, 1, 0:NSUB * E], tri[:], sel, start=True, stop=True)
                nc.tensor.matmul(psA[:, 1, NSUB * E:2 * NSUB * E], ones[:], sel, start=True, stop=True).then_inc(
                    pos_full, 1)

            def one_pass(k):
                pe.wait_ge(nrm_ready, k + 1)
                after(pe, slots_ready, k)
                for d in range(DC):
                    for s in range(NSUB):
                        ins = nc.tensor.transpose(psA[:, d, s * P:(s + 1) * P], nrm[:, s, d * P:(d + 1) * P], ident[:])
                    ins.then_inc(tr_full, 1)
                pe.wait_ge(nT_ready, k * DC + DC)
                for s in range(NSUB):
                    for d in range(DC):
                        ins = nc.tensor.matmul(psA[:, 0, s * E:(s + 1) * E], nT[:, d, s * P:(s + 1) * P], rwT[:, d, :],
                                               start=(d == 0), stop=(d == DC - 1))
                ins.then_inc(logit_full, 1)
                for m in range(HC):
                    up(k, m)
                    if m == HC // 2:
                        positions(k)
                    if m:
                        down(k, m - 1)
                down(k, HC - 1)

            one_pass(0)
            with pe.Fori(1, NT) as k:
                one_pass(k)

            pe.wait_ge(table_ready, 1)
            pe.wait_ge(s_w3, 2 * E * 16)

            def rows_T(i, par, turn):
                pe.wait_ge(xb_here[par], turn * 16 + 16)
                after(pe, nTb_ready, i)
                for d in range(DC):
                    ins = nc.tensor.transpose(psP[:, 0, d * P:(d + 1) * P], xb[:, par, d * P:(d + 1) * P], ident[:])
                ins.then_inc(T_done, 1)

            def expert_up(i, par):
                e = pe.value_load(block_exp[0:1, ds(i, 1)], min_val=0, max_val=E - 1)
                pe.wait_ge(nTb_ready, i + 1)
                after(pe, hs_ready, i)
                for a in range(2):
                    for d in range(DC):
                        ins = nc.tensor.matmul(psA[:, a, :], nTb[:, par, d, :], ew1_s[:, e, d, a * TC:(a + 1) * TC],
                                               start=(d == 0), stop=(d == DC - 1))
                ins.then_inc(A_done, 1)

            def hidden_T(i, par):
                pe.wait_ge(hs_ready, i + 1)
                after(pe, hb_ready, i)
                for m in range(HC):
                    ins = nc.tensor.transpose(psY[:, m // 4, (m % 4) * P:(m % 4 + 1) * P],
                                              hs[:, par, m * P:(m + 1) * P], ident[:])
                ins.then_inc(HT_done, 1)

            def expert_down(i, par):
                e = pe.value_load(block_exp[0:1, ds(i, 1)], min_val=0, max_val=E - 1)
                pe.wait_ge(hr_ready, i + 1)
                after(pe, eo_ready, i)
                for m in range(HC):
                    ins = nc.tensor.matmul(psP[:, 1, 0:O], hT[:, par, m, :], ew2_s[:, e, m, :],
                                           start=(m == 0), stop=(m == HC - 1))
                ins.then_inc(B_done, 1)

            rows_T(0, 0, 0)
            expert_up(0, 0)
            rows_T(1, 1, 0)
            def one_pass(t):
                for par in range(2):
                    i = t * 2 + par
                    hidden_T(i, par)
                    expert_up(i + 1, 1 - par)
                    expert_down(i, par)
                    rows_T(i + 2, par, t + 1)

            one_pass(0)
            with pe.Fori(1, NBLK // 2 - 1) as t:
                one_pass(t)
            hidden_T(NBLK - 2, 0)
            expert_up(NBLK - 1, 1)
            expert_down(NBLK - 2, 0)
            hidden_T(NBLK - 1, 1)
            expert_down(NBLK - 1, 1)


_INS = ['x', 'norm_scale', 'w_in', 'conv_w', 'conv_b', 'A_log', 'D', 'w_xproj', 'w_dt', 'b_dt', 'w_out']
_FFN = ['norm_weight', 'router_w', 'sw1', 'sb1', 'sw2', 'sb2', 'ew1', 'eb1', 'ew2', 'eb2']


def kernel(**inputs):
    import numpy as _np
    import concourse.bacc as _bacc
    from concourse import mybir as _mybir
    from concourse.bass_utils import run_bass_kernel_spmd as _run

    nc = _bacc.Bacc("TRN2", target_bir_lowering=False, num_devices=1)
    arrays, args = {}, []
    for name in ['L0_attn_' + n for n in _INS] + ['L0_ffn_' + n for n in _FFN]:
        a = _np.ascontiguousarray(inputs[name])
        arrays[f"in_{name}_dram"] = a
        args.append(nc.dram_tensor(f"in_{name}_dram", a.shape, _mybir.dt.from_np(a.dtype), kind="ExternalInput").ap())
    shape = inputs['L0_attn_x'].shape
    args.append(nc.dram_tensor("out_0_dram", shape, _mybir.dt.float32, kind="ExternalOutput").ap())
    build(nc, *args)
    r = _run(nc, [arrays], core_ids=[0])
    return r.results[0]["out_0_dram"]
```

```python
from contextlib import ExitStack

import concourse.bass as bass
from concourse import mybir

ALU = mybir.AluOpType
ACT = mybir.ActivationFunctionType
F32 = mybir.dt.float32
I32 = mybir.dt.int32
U32 = mybir.dt.uint32
AX_X = mybir.AxisListType.X
ds = bass.ds

P = 128
TC = 512
NSUB = TC // P


class Chain:

    def __init__(self, eng, sem):
        self.eng, self.sem, self.before, self.n = eng, sem, 0, 0

    def start(self, before):
        self.before, self.n = before, 0

    def done(self, instruction):
        instruction.then_inc(self.sem, 1)
        self.n += 1
        return self

    def wait(self):
        self.eng.wait_ge(self.sem, self.before + self.n)


def build(nc, x, norm_scale, w_in, conv_w, conv_b, A_log, D_skip, w_xproj, w_dt, b_dt, w_out,
          norm_weight, router_w, sw1, sb1, sw2, sb2, ew1, eb1, ew2, eb2, out):
    NB, L, D = x.shape
    T = NB * L
    NT = T // TC
    HALVES = L // TC
    NSUBS = T // P
    DI = w_in.shape[1] // 2
    CH = DI // P
    N = A_log.shape[1]
    R = w_dt.shape[0]
    K = conv_w.shape[0]
    DC = D // P
    E, H = eb1.shape
    HC = H // P
    O = ew2.shape[2]
    TOPK = 2
    MC = 2 * CH
    assert HALVES == 2 and D == O

    REGION = T + P
    NBLK = (TOPK * T + E * (P - 1)) // P
    NBLK += NBLK % 2
    SPARE = NBLK - TOPK * T // P
    ROWS = E * REGION + SPARE * P

    xt = x.rearrange("b l d -> (b l) d")
    ot = out.rearrange("b l d -> (b l) d")

    bc_dram = nc.dram_tensor("bc_dram", [2, 2 * N, TC], F32).ap()
    rows_dram = nc.dram_tensor("rows_dram", [ROWS, D], F32).ap()
    eo_dram = nc.dram_tensor("eo_dram", [NBLK * P, O], F32).ap()

    vec_parts = [("conv_w", conv_w.rearrange("k o (c p) -> (k o c) p", p=P), K * CH),
                 ("conv_b", conv_b.rearrange("(c p) -> c p", p=P), CH),
                 ("b_dt", b_dt.rearrange("(c p) -> c p", p=P), CH),
                 ("D", D_skip.rearrange("(c p) -> c p", p=P), CH),
                 ("norm_scale", norm_scale.rearrange("(c p) -> c p", p=P), DC),
                 ("norm_weight", norm_weight.rearrange("(c p) -> c p", p=P), DC),
                 ("sb1", sb1.rearrange("(c p) -> c p", p=P), HC),
                 ("eb1", eb1.rearrange("e (c p) -> (e c) p", p=P), E * HC)]
    vec_at, NV = {}, 0
    for name, _, n in vec_parts:
        vec_at[name] = NV
        NV += n
    assert NV <= P

    with ExitStack() as whole:
        def sem(name):
            return whole.enter_context(nc.semaphore(name))

        def alloc(ctx):
            return lambda name, shape, dt=F32: ctx.enter_context(nc.sbuf_tensor(name, shape, dt))

        sb = alloc(whole)
        xall = sb("xall", [P, NSUBS, D])
        ident = sb("ident", [P, P])
        vecs = sb("vecs", [P, NV])
        tri = sb("tri", [P, P])
        ones = sb("ones", [P, P])
        slots = sb("slots", [P, TOPK, NSUBS], U32)
        rows_of = sb("rows_of", [P, TOPK, NSUBS])
        wts = sb("wts", [P, TOPK, NSUBS])
        block_row = sb("block_row", [1, NBLK], I32)
        block_exp = sb("block_exp", [1, NBLK], I32)
        tail_row = sb("tail_row", [1, E], I32)
        psY = whole.enter_context(nc.psum_tensor("psY", [P, CH, TC], F32))
        psA = whole.enter_context(nc.psum_tensor("psA", [P, 2, TC], F32))
        psP = whole.enter_context(nc.psum_tensor("psP", [P, 2, TC], F32))

        def vec(name, i=0):
            a = vec_at[name] + i
            return vecs[:, a:a + 1]


        stage1 = ExitStack()
        sb = alloc(stage1)
        w_in_s = sb("w_in_s", [P, DC, 2 * DI])
        w_xp_s = sb("w_xp_s", [P, CH, R + 2 * N])
        w_dt_s = sb("w_dt_s", [R, DI])
        w_out_s = sb("w_out_s", [P, CH, D])
        convd = sb("convd", [P, K * CH, P])
        skipd = sb("skipd", [P, CH, P])
        A_s = sb("A_s", [P, CH, N])
        carry = sb("carry", [P, CH, N])
        rstd1 = sb("rstd1", [P, NSUBS])
        xr = sb("xr", [P, NSUB, D])
        xnT = sb("xnT", [P, DC, TC])
        xraw = sb("xraw", [P, CH, TC + K - 1])
        no_halo = sb("no_halo", [P, CH, K - 1])
        xs = sb("xs", [P, CH, TC])
        res = sb("res", [P, 2, CH, TC])
        delta = sb("delta", [P, 2, CH, TC])
        u = sb("u", [P, 2, CH, TC])
        spe = sb("spe", [P, CH, TC])
        spr = sb("spr", [P, CH, TC])
        proj = sb("proj", [R + 2 * N, TC])
        NX = 4
        X = sb("X", [P, NX, CH, TC])
        NBC = 4
        bc = sb("bc", [P, NBC, 2, TC])
        dA_s = sb("dA_s", [P, 2, TC])
        vrows = X[:, 0, 0, 0:P]
        stage1.close()

        stage2 = ExitStack()
        sb = alloc(stage2)
        ew2_s = sb("ew2_s", [P, E, HC, O])
        ew1_s = sb("ew1_s", [P, E, DC, H])
        stage2b = ExitStack()
        sb = alloc(stage2b)
        sw1_s = sb("sw1_s", [P, DC, H])
        sw2_s = sb("sw2_s", [P, HC, O])
        nrm = sb("nrm", [P, NSUB, D])
        nT = sb("nT", [P, DC, TC])
        NH = 2
        hT2 = sb("hT2", [P, NH, TC])
        sb2_s = sb("sb2_s", [P, O])
        junk = sb("junk", [P, D])
        rw = sb("rw", [E, D])
        rwT = sb("rwT", [P, DC, E])
        st6 = sb("st6", [P, NSUB, 6])
        mv = sb("mv", [P, NSUB, 2])
        sc = sb("sc", [P, 6, NSUB])
        prob = sb("prob", [P, NSUB, E])
        cmp = sb("cmp", [P, NSUB, E, E])
        cme = sb("cme", [P, NSUB, E, E])
        lower = sb("lower", [P, E, E])
        rank = sb("rank", [P, NSUB, E])
        top = sb("top", [P, TOPK + 1, NSUB, E])
        pick = sb("pick", [P, 2 * TOPK, NSUB, E])
        picked = sb("picked", [P, 2 * TOPK, NSUB])
        base = sb("base", [P, NSUB + 1, E])
        region = sb("region", [P, E])
        slot = sb("slot", [P, NSUB, E])
        slots_now = sb("slots_now", [P, TOPK, NSUB], U32)
        zero = sb("zero", [P, D])
        nblk = sb("nblk", [P, E])
        nblk_i = sb("nblk_i", [P, E], I32)
        cum = sb("cum", [P, E])
        shift = sb("shift", [P, 3, E])
        shifts = sb("shifts", [P, TOPK * NSUBS])
        row1 = sb("row1", [1, E])
        blk_no = sb("blk_no", [1, NBLK])
        passed = sb("passed", [1, 2, NBLK, E])
        bexp = sb("bexp", [1, 3, NBLK])
        stage2b.close()
        stage3 = ExitStack()
        sb = alloc(stage3)
        xb = sb("xb", [P, 2, D])
        nTb = sb("nTb", [P, 2, DC, P])
        hs = sb("hs", [P, 2, H])
        hT = sb("hT", [P, 2, HC, P])
        eo = sb("eo", [P, 2, O])
        eb2_s = sb("eb2_s", [P, E, O])
        stage3.close()
        stage2.close()
        stage4 = ExitStack()
        sb = alloc(stage4)
        slots4 = sb("slots4", [P, 2, TOPK, NSUB], U32)
        gat = sb("gat", [P, 2, NSUB, TOPK, D])
        st6f = sb("st6f", [P, 2, NSUB, 6])
        mvf = sb("mvf", [P, 2, NSUB, 2])
        scf = sb("scf", [P, 2, 2, NSUB])
        fin = sb("fin", [P, 2, NSUB, D])
        stage4.close()

        s_const = sem("s_const")
        s_w1 = sem("s_w1")
        s_x = sem("s_x")
        s_vecT = sem("s_vecT")
        s_vecs = sem("s_vecs")
        s_setup = sem("s_setup")
        s_ssq = sem("s_ssq")
        xr_ready = sem("xr_ready")
        p_full = sem("p_full")
        p_free = [sem(f"p_free{i}") for i in range(2)]
        halo_ready = sem("halo_ready")
        bcw_done = sem("bcw_done")
        bc_here = [sem(f"bc_here{i}") for i in range(NBC)]
        xs_ready = sem("xs_ready")
        res_ready = sem("res_ready")
        r_ready = sem("r_ready")
        e_ready = sem("e_ready")
        l_ready = sem("l_ready")
        t1_ready = sem("t1_ready")
        sp_link = sem("sp_link")
        delta_ready = sem("delta_ready")
        u_ready = sem("u_ready")
        bx_ready = sem("bx_ready")
        dA_ready = sem("dA_ready")
        scan_done = sem("scan_done")
        carry_done = sem("carry_done")
        hc_ready = sem("hc_ready")
        y_acc = sem("y_acc")
        z_done = sem("z_done")

        s_c2 = sem("s_c2")
        s_passed = sem("s_passed")
        s_w2 = sem("s_w2")
        s_w3 = sem("s_w3")
        rwT_full = sem("rwT_full")
        rwT_ready = sem("rwT_ready")
        v_ready = sem("v_ready")
        sq_ready = sem("sq_ready")
        x2_ready = sem("x2_ready")
        ss_ready = sem("ss_ready")
        nrm_ready = sem("nrm_ready")
        d_link = sem("d_link")
        tr_full = sem("tr_full")
        nT_ready = sem("nT_ready")
        logit_full = sem("logit_full")
        prob_ready = sem("prob_ready")
        sel_ready = sem("sel_ready")
        pos_full = sem("pos_full")
        slots_ready = sem("slots_ready")
        scattered = sem("scattered")
        h_full = sem("h_full")
        relu_done = sem("relu_done")
        o_done = sem("o_done")
        acc_done = sem("acc_done")
        table_ready = sem("table_ready")
        zeroed = sem("zeroed")
        s_eb2 = sem("s_eb2")
        xb_here = [sem(f"xb_here{i}") for i in range(2)]
        T_done = sem("T_done")
        nTb_ready = sem("nTb_ready")
        A_done = sem("A_done")
        hs_ready = sem("hs_ready")
        HT_done = sem("HT_done")
        hb_ready = sem("hb_ready")
        hr_ready = sem("hr_ready")
        B_done = sem("B_done")
        eo_ready = sem("eo_ready")
        eo_out = [sem(f"eo_out{i}") for i in range(2)]
        slots4_ready = sem("slots4_ready")
        gathered = [sem(f"gathered{i}") for i in range(2)]
        v4_ready = sem("v4_ready")
        sq4_ready = sem("sq4_ready")
        f_link = sem("f_link")
        fin_ready = sem("fin_ready")
        out_done = [sem(f"out_done{i}") for i in range(2)]

        block = whole.enter_context(nc.Block())

        ORDER = ([("T", d) for d in range(DC)] + [("I", m) for m in range(CH)] + [("C", c) for c in range(CH)]
                 + [("I", CH), ("X", 0)] + [("D", c) for c in range(CH)]
                 + [("I", m) for m in range(CH + 1, MC)] + [("O", 0), ("O", 1)])
        USES = len(ORDER)
        assert USES % 2 == 1

        def place(b, half, use):
            if use[0] != "O":
                return half * USES + ORDER.index(use)
            if isinstance(b, int) and (b, half) == (NB - 1, 1):
                return half * USES + ORDER.index(use) + 2
            return (half + 1) * USES + ORDER.index(use)

        def skipped(b, half, use):
            return 0 if isinstance(b, int) and b == 0 and half == 0 and use[0] != "O" else 1

        def bank_of(b, half, use):
            return place(b, half, use) % 2

        def uses_before(b, half, use):
            return b * USES + (place(b, half, use) // 2 - skipped(b, half, use))

        def tile_count(b, half, per, add=0):
            return b * (2 * per) + (half * per + add)

        def pwait(eng, b, half, use):
            eng.wait_ge(p_full, b * (2 * USES) + (place(b, half, use) + 1 - 2 * skipped(b, half, use)))
            return psP[:, bank_of(b, half, use), :]

        def evacuated(eng, b, half, *uses):
            for use in uses:
                eng.wait_ge(p_free[bank_of(b, half, use)], uses_before(b, half, use) + 1)

        def decay_of(c):
            return psA[:, c, :] if c < 2 else dA_s[:, c - 2, :]

        def following(b, half):
            return (b, 1) if half == 0 else (b + 1, 0)

        def previous(b, half):
            return (b, 0) if half == 1 else (b - 1, 1)

        def settled(eng):
            eng.sem_inc(s_passed, 1)

        def after(eng, sem, count):
            if not isinstance(count, int) or count > 0:
                eng.wait_ge(sem, count)

        def stage1_over(eng):
            for i in range(2):
                eng.wait_ge(p_free[i], NT * USES // 2)

        def stage3_over(eng):
            for i in range(2):
                eng.wait_ge(eo_out[i], 16 * (NBLK // 2))

        FRONT = 4
        LINKS2 = 31
        LINKS4 = 17
        W1_DMAS = len(vec_parts) + 5
        SETUP = 3 + K * CH + CH + 1
        UBC = [len(range(i, N, NBC)) for i in range(NBC)]

        @block.gpsimd
        def _(pool):
            nc.gpsimd.memset(ident[:], 0.0).then_inc(s_const, 1)
            nc.gpsimd.memset(tri[:], 1.0).then_inc(s_const, 1)
            nc.gpsimd.memset(ones[:], 1.0).then_inc(s_const, 1)
            pool.wait_ge(s_const, 3)
            nc.gpsimd.affine_select(out=ident[:], in_=ident[:], compare_op=ALU.not_equal, fill=1.0, base=0,
                                    pattern=[[-1, P]], channel_multiplier=1).then_inc(s_const, 1)
            nc.gpsimd.affine_select(out=tri[:], in_=tri[:], compare_op=ALU.is_gt, fill=0.0, base=0,
                                    pattern=[[1, P]], channel_multiplier=-1).then_inc(s_const, 1)

            def correct(b, half):
                pool.wait_ge(t1_ready, tile_count(b, half, 1, 1))
                pool.wait_ge(l_ready, tile_count(b, half, 1, 1))
                nc.gpsimd.tensor_tensor(spe[:], spe[:], delta[:, half], ALU.subtract).then_inc(sp_link, 1)

            def softplus_sum(b, half):
                pool.wait_ge(sp_link, tile_count(b, half, 1, 1))
                pool.wait_ge(r_ready, tile_count(b, half, 1, 1))
                nc.gpsimd.tensor_tensor(delta[:, half], spr[:], spe[:], ALU.add).then_inc(delta_ready, 1)

            def input_scale(b, half):
                pool.wait_ge(delta_ready, tile_count(b, half, 1, 1))
                nc.gpsimd.tensor_tensor(u[:, half], delta[:, half], xs[:], ALU.mult).then_inc(u_ready, 1)

            def input_step(b, half, n):
                if n == 0:
                    pool.wait_ge(u_ready, tile_count(b, half, 1, 1))
                pool.wait_ge(bc_here[n % NBC], tile_count(b, half, 16 * UBC[n % NBC], 16 * (n // NBC + 1)))
                after(pool, y_acc, tile_count(b, half, N, n - NX + 1))
                nc.gpsimd.tensor_tensor(X[:, n % NX], u[:, half],
                                        bc[:, n % NBC, 0:1, :].broadcast_to([P, CH, TC]),
                                        ALU.mult).then_inc(bx_ready, 1)

            def period(b, half, first=False, last=False):
                for n in range(N):
                    input_step(b, half, n)
                if not last:
                    for stage in (correct, softplus_sum, input_scale):
                        stage(*following(b, half))

            for stage in (correct, softplus_sum, input_scale):
                stage(0, 0)
            period(0, 0, first=True)
            period(0, 1)
            with pool.Fori(1, NB - 1) as b:
                for half in range(HALVES):
                    period(b, half)
            period(NB - 1, 0)
            period(NB - 1, 1, last=True)

            stage1_over(pool)
            nc.gpsimd.memset(lower[:], 1.0).then_inc(s_c2, 1)
            nc.gpsimd.memset(zero[:], 0.0).then_inc(s_c2, 1)
            nc.gpsimd.memset(base[:, 0, :], 0.0).then_inc(s_c2, 1)
            nc.gpsimd.iota(region[:], pattern=[[REGION, E]], base=0, channel_multiplier=0,
                           allow_small_or_imprecise_dtypes=True).then_inc(s_c2, 1)
            nc.gpsimd.iota(blk_no[:], pattern=[[1, NBLK]], base=0, channel_multiplier=0,
                           allow_small_or_imprecise_dtypes=True).then_inc(s_c2, 1)
            pool.wait_ge(s_c2, 5)
            nc.gpsimd.affine_select(out=lower[:], in_=lower[:], compare_op=ALU.is_gt, fill=0.0, base=0,
                                    pattern=[[1, E], [-1, E]], channel_multiplier=0).then_inc(s_c2, 1)
            def one_pass(k):
                pool.wait_ge(nrm_ready, k + 1)
                pool.wait_ge(slots_ready, k + 1)
                settled(pool)
                for j in range(TOPK):
                    for s in range(NSUB):
                        nc.gpsimd.indirect_dma_start(
                            out=rows_dram, out_offset=bass.IndirectOffsetOnAxis(ap=slots_now[:, j, s:s + 1], axis=0),
                            in_=nrm[:, s, :], in_offset=None).then_inc(scattered, 16)

            one_pass(0)
            with pool.Fori(1, NT) as k:
                one_pass(k)

            def gather(b, half):
                pool.wait_ge(slots4_ready, b * HALVES + (half + 1))
                settled(pool)
                for s in range(NSUB):
                    for j in range(TOPK):
                        nc.gpsimd.indirect_dma_start(
                            out=gat[:, half, s, j, :], out_offset=None, in_=eo_dram,
                            in_offset=bass.IndirectOffsetOnAxis(ap=slots4[:, half, j, s:s + 1], axis=0)).then_inc(
                            gathered[half], 16)

            stage3_over(pool)
            def one_pass(b):
                for half in range(HALVES):
                    gather(b, half)

            one_pass(0)
            with pool.Fori(1, NB) as b:
                one_pass(b)

        @block.sync
        def _(sp):
            sp.dma_start(xall[:], xt.rearrange("(t p) d -> p t d", p=P)).then_inc(s_x, 16)
            for name, src, n in vec_parts:
                sp.dma_start(vrows[vec_at[name]:vec_at[name] + n, :], src).then_inc(s_w1, 16)
            sp.dma_start(A_s[:], A_log.rearrange("(c p) n -> p c n", p=P)).then_inc(s_w1, 16)
            sp.dma_start(w_in_s[:], w_in.rearrange("(c p) n -> p c n", p=P)).then_inc(s_w1, 16)
            sp.dma_start(w_xp_s[:], w_xproj.rearrange("(c p) n -> p c n", p=P)).then_inc(s_w1, 16)
            sp.dma_start(w_dt_s[:], w_dt).then_inc(s_w1, 16)
            sp.dma_start(w_out_s[:], w_out.rearrange("(c p) n -> p c n", p=P)).then_inc(s_w1, 16)

            def store_bc(b, half):
                evacuated(sp, b, half, ("X", 0))
                sp.dma_start(bc_dram[half], proj[R:R + 2 * N, :]).then_inc(bcw_done, 16)

            def load_bc(b, half, n):
                after(sp, hc_ready, tile_count(b, half, N, n - NBC + 1))
                src = bc_dram[half].rearrange("(w n) t -> n w t", w=2)[n:n + 1]
                sp.dma_start(bc[:, n % NBC], src.broadcast_to([P, 2, TC])).then_inc(bc_here[n % NBC], 16)

            def period(b, half, first=False, last=False):
                sp.wait_ge(bcw_done, tile_count(b, half, 16, 16))
                settled(sp)
                for n in range(N):
                    load_bc(b, half, n)
                    if n == 10 and not last:
                        store_bc(*following(b, half))

            store_bc(0, 0)
            period(0, 0, first=True)
            period(0, 1)
            with sp.Fori(1, NB - 1) as b:
                for half in range(HALVES):
                    period(b, half)
            period(NB - 1, 0)
            period(NB - 1, 1, last=True)

            stage1_over(sp)
            sp.dma_start(rw[:], router_w).then_inc(s_w2, 16)
            sp.dma_start(sw1_s[:], sw1.rearrange("(c p) n -> p c n", p=P)).then_inc(s_w2, 16)
            sp.dma_start(sw2_s[:], sw2.rearrange("(c p) n -> p c n", p=P)).then_inc(s_w2, 16)
            sp.dma_start(sb2_s[:], sb2.rearrange("(a n) -> a n", a=1).broadcast_to([P, O])).then_inc(s_w2, 16)
            for e in range(E):
                sp.dma_start(ew1_s[:, e], ew1[e].rearrange("(c p) n -> p c n", p=P)).then_inc(s_w3, 16)
                sp.dma_start(ew2_s[:, e], ew2[e].rearrange("(c p) n -> p c n", p=P)).then_inc(s_w3, 16)
            sp.wait_ge(s_c2, 6)
            for i in range(SPARE):
                sp.dma_start(rows_dram[E * REGION + i * P:E * REGION + (i + 1) * P, :], zero[:]).then_inc(zeroed, 16)
            sp.wait_ge(table_ready, 1)
            with sp.Fori(0, E) as e:
                row = sp.value_load(tail_row[0:1, ds(e, 1)], min_val=0, max_val=(E - 1) * REGION + T)
                sp.dma_start(rows_dram[ds(row, P), :], zero[:]).then_inc(zeroed, 16)
            sp.wait_ge(zeroed, 16 * (SPARE + E))
            sp.wait_ge(scattered, 16 * TOPK * NSUBS)
            sp.dma_start(eb2_s[:], eb2.rearrange("(a e) n -> a e n", a=1).broadcast_to([P, E, O])).then_inc(s_eb2, 16)

            def load_block(i, par):
                row = sp.value_load(block_row[0:1, ds(i, 1)], min_val=0, max_val=ROWS - P)
                sp.dma_start(xb[:, par, :], rows_dram[ds(row, P), :]).then_inc(xb_here[par], 16)

            def store_block(i, par):
                sp.wait_ge(eo_ready, i + 1)
                sp.dma_start(eo_dram[ds(i * P, P), :], eo[:, par, :]).then_inc(eo_out[par], 16)

            for i in range(2):
                load_block(i, i)
            def one_pass(t):
                for par in range(2):
                    sp.wait_ge(T_done, t * 2 + (par + 1))
                    load_block(t * 2 + (par + 2), par)
                    store_block(t * 2 + par, par)

            one_pass(0)
            with sp.Fori(1, NBLK // 2 - 1) as t:
                one_pass(t)
            for par in range(2):
                store_block(NBLK - 2 + par, par)

            def one_pass(b):
                for half in range(HALVES):
                    sp.wait_ge(fin_ready, b * HALVES + (half + 1))
                    sp.dma_start(ot.rearrange("(t p) d -> p t d", p=P)[:, ds(b * (HALVES * NSUB) + half * NSUB, NSUB), :],
                                 fin[:, half]).then_inc(out_done[half], 16)

            one_pass(0)
            with sp.Fori(1, NB) as b:
                one_pass(b)
            for half in range(HALVES):
                sp.wait_ge(out_done[half], 16 * NB)

        @block.scalar
        def _(act):
            act.wait_ge(s_x, 16)
            for t in range(NSUBS):
                ins = nc.scalar.activation(spe[:, 0, 0:D], xall[:, t, :], ACT.Square,
                                           accum_out=rstd1[:, t:t + 1]).then_inc(s_ssq, 1)
                act.wait_ge(s_ssq, t + 1)
            act.wait_ge(s_setup, 1)
            nc.scalar.activation(rstd1[:], rstd1[:], ACT.Sqrt).then_inc(s_ssq, 1)
            act.wait_ge(s_w1, W1_DMAS * 16)
            nc.scalar.activation(A_s[:], A_s[:], ACT.Exp).then_inc(s_ssq, 1)
            act.wait_ge(s_vecT, 1)
            nc.scalar.activation(vecs[:], psP[:, 0, 0:NV], ACT.Copy).then_inc(s_vecs, 1)
            act.wait_ge(s_vecs, 1)
            act.wait_ge(s_setup, SETUP)

            def read(b, half, use, out_, func, rows=P, **kw):
                src = pwait(act, b, half, use)[0:rows, :]
                nc.scalar.activation(out_, src, func, **kw).then_inc(p_free[bank_of(b, half, use)], 1)

            def read_rows(b, half, d):
                read(b, half, ("T", d), xnT[:, d, :], ACT.Copy, scale=vec("norm_scale", d))

            def read_in(b, half, m):
                if m < CH:
                    read(b, half, ("I", m), xraw[:, m, K - 1:], ACT.Copy)
                else:
                    read(b, half, ("I", m), res[:, half, m - CH, :], ACT.Copy)

            def halo(b, half):
                if not (isinstance(b, int) and b == 0 and half == 0):
                    evacuated(act, *previous(b, half), ("C", CH - 2), ("C", CH - 1))
                nc.scalar.activation(xraw[:, :, 0:K - 1], xraw[:, :, TC:TC + K - 1] if half else no_halo[:],
                                     ACT.Copy).then_inc(halo_ready, 1)
                act.wait_ge(halo_ready, tile_count(b, half, 1, 1))

            def read_conv(b, half, c):
                if c == 0:
                    after(act, u_ready, tile_count(b, half, 1, 0))
                read(b, half, ("C", c), xs[:, c, :], ACT.Identity, bias=vec("conv_b", c))

            def silu_xs(b, half):
                evacuated(act, b, half, ("C", CH - 2), ("C", CH - 1))
                nc.scalar.activation(xs[:], xs[:], ACT.Silu).then_inc(xs_ready, 1)

            def silu_gate(b, half):
                evacuated(act, b, half, ("I", MC - 2), ("I", MC - 1))
                nc.scalar.activation(res[:, half], res[:, half], ACT.Silu).then_inc(res_ready, 1)

            def read_proj(b, half):
                read(b, half, ("X", 0), proj[:], ACT.Copy, rows=R + 2 * N)

            def read_dt(b, half, c):
                src = pwait(act, b, half, ("D", c))
                nc.scalar.activation(spe[:, c, :], src, ACT.Abs, bias=vec("b_dt", c))
                read(b, half, ("D", c), spr[:, c, :], ACT.Relu, bias=vec("b_dt", c))

            def exp_ln(b, half):
                evacuated(act, b, half, ("D", CH - 2), ("D", CH - 1))
                nc.scalar.activation(spe[:], spe[:], ACT.Exp, scale=-1.0).then_inc(e_ready, 1)
                act.wait_ge(e_ready, tile_count(b, half, 1, 1))
                nc.scalar.activation(u[:, half], spe[:], ACT.Ln, bias=1.0).then_inc(l_ready, 1)

            ACT_PARTS = {(1, 1): [(read_rows, 0)], (1, 3): [(read_rows, 1)],
                         (2, 1): [(halo,), (read_in, 0)], (2, 3): [(read_in, 1)],
                         (3, 1): [(read_in, 2)], (3, 3): [(read_in, 3)],
                         (4, 3): [(read_conv, 0)], (5, 3): [(read_conv, 1)], (6, 3): [(read_conv, 2)],
                         (7, 3): [(read_conv, 3), (silu_xs,)],
                         (8, 3): [(read_in, 4)],
                         (9, 3): [(read_proj,)],
                         (10, 1): [(read_dt, 0)], (10, 3): [(read_dt, 1)],
                         (11, 1): [(read_dt, 2)], (11, 3): [(read_dt, 3), (exp_ln,)],
                         (12, 3): [(read_in, 5)], (13, 3): [(read_in, 6)],
                         (14, 3): [(read_in, 7),]}

            GATE_AT = (7, 3)

            def prep_part(at, b, half):
                for part, *which in ACT_PARTS.get(at, ()):
                    part(b, half, *which)

            def decay(b, half, n, c):
                if n == 0 and c == 0:
                    act.wait_ge(delta_ready, tile_count(b, half, 1, 1))
                v = n * CH + c
                after(act, scan_done, tile_count(b, half, N * CH, v - CH + 1 if v >= CH else 0))
                nc.scalar.activation(decay_of(c), delta[:, half, c, :], ACT.Exp,
                                     scale=A_s[:, c, n:n + 1]).then_inc(dA_ready, 1)

            def period(b, half, first=False, last=False):
                for n in range(N):
                    for c in range(CH):
                        decay(b, half, n, c)
                        if not last:
                            prep_part((n, c), *following(b, half))
                        if (n, c) == GATE_AT:
                            silu_gate(b, half)

            for at in sorted(ACT_PARTS):
                prep_part(at, 0, 0)
            period(0, 0, first=True)
            period(0, 1)
            with act.Fori(1, NB - 1) as b:
                for half in range(HALVES):
                    period(b, half)
            period(NB - 1, 0)
            period(NB - 1, 1, last=True)

            stage1_over(act)
            act.wait_ge(rwT_full, 1)
            nc.scalar.activation(rwT[:], psA[:, 0, 0:DC * E].rearrange("p (c e) -> p c e", c=DC),
                                 ACT.Copy).then_inc(rwT_ready, 1)

            def norm_root(k):
                act.wait_ge(v_ready, k * 2 + 1)
                nc.scalar.activation(sc[:, 1, :], sc[:, 0, :], ACT.Sqrt).then_inc(sq_ready, 1)

            def squares(k):
                act.wait_ge(x2_ready, k + 1)
                for s in range(NSUB):
                    nc.scalar.activation(junk[:], xall[:, k * NSUB + s, :], ACT.Square,
                                         accum_out=sc[:, 3, s:s + 1]).then_inc(ss_ready, 1)
                    act.wait_ge(ss_ready, k * NSUB + (s + 1))

            def rms_root(k):
                act.wait_ge(v_ready, k * 2 + 2)
                nc.scalar.activation(sc[:, 5, :], sc[:, 4, :], ACT.Sqrt).then_inc(sq_ready, 1)

            def read_router(k):
                for d in range(DC):
                    act.wait_ge(tr_full, k * DC + (d + 1))
                    nc.scalar.activation(nT[:, d, :], psA[:, d, :], ACT.Copy,
                                         scale=vec("norm_weight", d)).then_inc(nT_ready, 1)
                act.wait_ge(logit_full, k + 1)
                nc.scalar.activation(prob[:], psA[:, 0, 0:NSUB * E].rearrange("p (s e) -> p s e", s=NSUB),
                                     ACT.Exp, scale=-1.0).then_inc(prob_ready, 1)

            def one_pass(k, last=False):
                for m in range(HC):
                    act.wait_ge(h_full, k * HC + (m + 1))
                    after(act, o_done, k * HC + max(m - 1, 0))
                    nc.scalar.activation(hT2[:, m % NH, :], psP[:, m % 2, :], ACT.Relu,
                                         bias=vec("sb1", m)).then_inc(relu_done, 1)
                    if m in ROOTS and not last:
                        ROOTS[m](k + 1)
                if not last:
                    read_router(k + 1)

            ROOTS = {HC - 4: norm_root, HC - 3: squares, HC - 2: rms_root}
            for part in (norm_root, squares, rms_root, read_router):
                part(0)
            one_pass(0)
            with act.Fori(1, NT - 1) as k:
                one_pass(k)
            one_pass(NT - 1, last=True)

            def scale_rows(i, par):
                act.wait_ge(T_done, i + 1)
                for d in range(DC):
                    ins = nc.scalar.activation(nTb[:, par, d, :], psP[:, 0, d * P:(d + 1) * P], ACT.Copy,
                                               scale=vec("norm_weight", d))
                ins.then_inc(nTb_ready, 1)

            def relu(i, par):
                act.wait_ge(hb_ready, i + 1)
                nc.scalar.activation(hT[:, par], hT[:, par], ACT.Relu).then_inc(hr_ready, 1)

            for i in range(2):
                scale_rows(i, i)
            def one_pass(t):
                for par in range(2):
                    relu(t * 2 + par, par)
                    scale_rows(t * 2 + (par + 2), par)

            one_pass(0)
            with act.Fori(1, NBLK // 2 - 1) as t:
                one_pass(t)
            for par in range(2):
                relu(NBLK - 2 + par, par)

            def one_pass(b):
                for half in range(HALVES):
                    act.wait_ge(v4_ready, b * HALVES + (half + 1))
                    nc.scalar.activation(scf[:, half, 1, :], scf[:, half, 0, :], ACT.Sqrt).then_inc(sq4_ready, 1)

            one_pass(0)
            with act.Fori(1, NB) as b:
                one_pass(b)

        @block.vector
        def _(dve):
            dve.wait_ge(s_ssq, NSUBS)
            nc.vector.tensor_scalar(rstd1[:], rstd1[:], 1.0 / D, 1e-5, ALU.mult, ALU.add).then_inc(s_setup, 1)
            dve.wait_ge(s_ssq, NSUBS + 1)
            nc.vector.reciprocal(rstd1[:], rstd1[:]).then_inc(s_setup, 1)
            dve.wait_ge(s_ssq, NSUBS + 2)
            nc.vector.tensor_scalar(A_s[:], A_s[:], -1.0, None, ALU.mult).then_inc(s_setup, 1)
            dve.wait_ge(s_vecs, 1)
            for i in range(K * CH):
                nc.vector.tensor_scalar(convd[:, i, :], ident[:], vec("conv_w", i), None, ALU.mult).then_inc(s_setup, 1)
            for c in range(CH):
                nc.vector.tensor_scalar(skipd[:, c, :], ident[:], vec("D", c), None, ALU.mult).then_inc(s_setup, 1)
            nc.vector.memset(no_halo[:], 0.0).then_inc(s_setup, 1)
            dve.wait_ge(s_setup, SETUP)

            def norm_rows(b, half, before=None):
                k = b * HALVES + half
                if before:
                    pwait(dve, *before, ("T", DC - 1))
                for s in range(NSUB):
                    ins = nc.vector.tensor_scalar(xr[:, s, :], xall[:, k * NSUB + s, :],
                                                  rstd1[:, ds(k * NSUB + s, 1)], None, ALU.mult)
                ins.then_inc(xr_ready, 1)

            def one_plus_e(b, half):
                dve.wait_ge(e_ready, tile_count(b, half, 1, 1))
                nc.vector.tensor_scalar(delta[:, half], spe[:], 1.0, -1.0, ALU.add, ALU.add).then_inc(t1_ready, 1)

            def relu_plus_ln(b, half):
                dve.wait_ge(l_ready, tile_count(b, half, 1, 1))
                nc.vector.tensor_tensor(spr[:], spr[:], u[:, half], ALU.add).then_inc(r_ready, 1)

            def scan(b, half, n, c):
                dve.wait_ge(dA_ready, tile_count(b, half, N * CH, n * CH + c + 1))
                start = carry[:, c, n:n + 1] if half else 0.0
                nc.vector.tensor_tensor_scan(X[:, n % NX, c, :], decay_of(c), X[:, n % NX, c, :], start,
                                             ALU.mult, ALU.add).then_inc(scan_done, 1)

            def keep_state(b, half, n):
                dve.wait_ge(scan_done, tile_count(b, half, N * CH, (n + 1) * CH))
                nc.vector.tensor_copy(carry[:, :, n:n + 1], X[:, n % NX, :, TC - 1:TC]).then_inc(carry_done, 1)

            def output_step(b, half, n):
                dve.wait_ge(scan_done, tile_count(b, half, N * CH, (n + 1) * CH))
                if half == 0:
                    dve.wait_ge(carry_done, b * N + (n + 1))
                nc.vector.tensor_tensor(X[:, n % NX], X[:, n % NX],
                                        bc[:, n % NBC, 1:2, :].broadcast_to([P, CH, TC]),
                                        ALU.mult).then_inc(hc_ready, 1)

            def step(b, half, n):
                dve.wait_ge(bx_ready, tile_count(b, half, N, n + 1))
                if half and n == 0:
                    dve.wait_ge(carry_done, b * N + N)
                for c in range(CH):
                    scan(b, half, n, c)
                    if c == 0 and n and half == 0:
                        keep_state(b, half, n - 1)
                    if c == 1 and n:
                        output_step(b, half, n - 1)

            def gate(b, half):
                dve.wait_ge(y_acc, tile_count(b, half, N, N))
                dve.wait_ge(res_ready, tile_count(b, half, 1, 1))
                nc.vector.tensor_tensor(res[:, half], psY[:], res[:, half], ALU.mult).then_inc(z_done, 1)

            def residual(b, half):
                k = b * HALVES + half
                for j in range(2):
                    src = pwait(dve, b, half, ("O", j)).rearrange("p (s d) -> p s d", s=2)
                    rows = xall[:, ds(k * NSUB + 2 * j, 2), :]
                    nc.vector.scalar_tensor_tensor(out=rows, in0=rows, scalar=2.0, in1=src,
                                                   op0=ALU.mult, op1=ALU.add).then_inc(
                        p_free[bank_of(b, half, ("O", j))], 1)

            def period(b, half, first=False, last=False):
                if not last:
                    norm_rows(*following(b, half), before=(b, half))
                for n in range(N):
                    step(b, half, n)
                    if n == 0 and not first:
                        residual(*previous(b, half))
                    if n == 11 and not last:
                        one_plus_e(*following(b, half))
                    if n == 12 and not last:
                        relu_plus_ln(*following(b, half))
                if half == 0:
                    keep_state(b, half, N - 1)
                output_step(b, half, N - 1)
                gate(b, half)

            norm_rows(0, 0)
            one_plus_e(0, 0)
            relu_plus_ln(0, 0)
            period(0, 0, first=True)
            period(0, 1)
            with dve.Fori(1, NB - 1) as b:
                for half in range(HALVES):
                    period(b, half)
            period(NB - 1, 0)
            period(NB - 1, 1, last=True)
            residual(NB - 1, 1)

            stage1_over(dve)
            dve.wait_ge(s_c2, 6)
            dve.wait_ge(s_w2, 4 * 16)
            link = Chain(dve, d_link)

            def norms(k):
                def row(s):
                    return xall[:, k * NSUB + s, :]

                settled(dve)
                for s in range(NSUB):
                    ins = nc.vector.bn_stats(out=st6[:, s, :], in_=row(s))
                link.done(ins).wait()
                settled(dve)
                for s in range(NSUB):
                    ins = nc.vector.bn_aggr(out=mv[:, s, :], in_=st6[:, s, :])
                link.done(ins).wait()
                nc.vector.tensor_scalar(sc[:, 0, :], mv[:, :, 1], 1e-5, None, ALU.add).then_inc(v_ready, 1)
                dve.wait_ge(sq_ready, k * 2 + 1)
                link.done(nc.vector.reciprocal(sc[:, 2, :], sc[:, 1, :])).wait()
                for s in range(NSUB):
                    ins = nc.vector.tensor_scalar(row(s), row(s), mv[:, s, 0:1], sc[:, 2, s:s + 1],
                                                  ALU.subtract, ALU.mult)
                ins.then_inc(x2_ready, 1)
                dve.wait_ge(ss_ready, k * NSUB + NSUB)
                nc.vector.tensor_scalar(sc[:, 4, :], sc[:, 3, :], 1.0 / D, 1e-8, ALU.mult, ALU.add).then_inc(v_ready, 1)
                dve.wait_ge(sq_ready, k * 2 + 2)
                link.done(nc.vector.reciprocal(sc[:, 5, :], sc[:, 5, :])).wait()
                after(dve, scattered, k * (16 * TOPK * NSUB))
                dve.wait_ge(x2_ready, k + 1)
                for s in range(NSUB):
                    ins = nc.vector.tensor_scalar(nrm[:, s, :], row(s), sc[:, 5, s:s + 1], None, ALU.mult)
                ins.then_inc(nrm_ready, 1)

            def select(k):
                rows = xall[:, ds(k * NSUB, NSUB), :]
                dve.wait_ge(prob_ready, k + 1)
                link.done(nc.vector.tensor_tensor(rows, rows, sb2_s[:].unsqueeze(1).broadcast_to([P, NSUB, O]), ALU.add))
                link.done(nc.vector.tensor_scalar(prob[:], prob[:], 1.0, None, ALU.add)).wait()
                link.done(nc.vector.reciprocal(prob[:], prob[:])).wait()
                p_j = prob[:].unsqueeze(2).broadcast_to([P, NSUB, E, E])
                p_e = prob[:].unsqueeze(3).broadcast_to([P, NSUB, E, E])
                link.done(nc.vector.tensor_tensor(cme[:], p_j, p_e, ALU.is_equal))
                link.done(nc.vector.tensor_tensor(cmp[:], p_j, p_e, ALU.is_gt)).wait()
                link.done(nc.vector.tensor_tensor(cme[:], cme[:], lower[:].unsqueeze(1).broadcast_to([P, NSUB, E, E]),
                                                  ALU.mult)).wait()
                link.done(nc.vector.tensor_tensor(cmp[:], cmp[:], cme[:], ALU.add)).wait()
                link.done(nc.vector.tensor_reduce(rank[:], cmp[:], AX_X, ALU.add)).wait()
                nc.vector.tensor_scalar(top[:, TOPK], rank[:], TOPK - 0.5, None, ALU.is_lt).then_inc(sel_ready, 1)
                for j in range(TOPK):
                    link.done(nc.vector.tensor_scalar(top[:, j], rank[:], float(j), None, ALU.is_equal))
                link.wait()
                for j in range(TOPK):
                    link.done(nc.vector.tensor_tensor(pick[:, j], prob[:], top[:, j], ALU.mult))
                dve.wait_ge(pos_full, k + 1)
                for s in range(NSUB):
                    link.done(nc.vector.tensor_tensor(base[:, s + 1, :], base[:, s, :],
                                                      psA[:, 1, (NSUB + s) * E:(NSUB + s + 1) * E], ALU.add)).wait()
                link.done(nc.vector.tensor_tensor(slot[:], base[:, 0:NSUB, :],
                                                  psA[:, 1, 0:NSUB * E].rearrange("p (s e) -> p s e", s=NSUB),
                                                  ALU.add)).wait()
                link.done(nc.vector.tensor_tensor(slot[:], slot[:], region[:].unsqueeze(1).broadcast_to([P, NSUB, E]),
                                                  ALU.add))
                link.done(nc.vector.tensor_copy(base[:, 0, :], base[:, NSUB, :])).wait()
                for j in range(TOPK):
                    link.done(nc.vector.tensor_tensor(pick[:, TOPK + j], slot[:], top[:, j], ALU.mult))
                link.wait()
                link.done(nc.vector.tensor_reduce(picked[:], pick[:], AX_X, ALU.add)).wait()
                nc.vector.tensor_copy(slots_now[:], picked[:, TOPK:]).then_inc(slots_ready, 1)
                link.done(nc.vector.tensor_copy(rows_of[:, :, ds(k * NSUB, NSUB)], picked[:, TOPK:]))
                link.done(nc.vector.tensor_tensor(sc[:, 0, :], picked[:, 0], picked[:, 1], ALU.add)).wait()
                link.done(nc.vector.tensor_scalar(sc[:, 0, :], sc[:, 0, :], 1e-6, None, ALU.add)).wait()
                link.done(nc.vector.reciprocal(sc[:, 0, :], sc[:, 0, :])).wait()
                link.done(nc.vector.tensor_tensor(wts[:, :, ds(k * NSUB, NSUB)], picked[:, 0:TOPK],
                                                  sc[:, 0:1, :].broadcast_to([P, TOPK, NSUB]), ALU.mult)).wait()

            def add_shared(k):
                dve.wait_ge(o_done, k * HC + HC)
                rows = xall[:, ds(k * NSUB, NSUB), :]
                nc.vector.tensor_tensor(rows, rows, psY[:, :, 0:O], ALU.add).then_inc(acc_done, 1)

            def one_pass(k, last=False):
                link.start(k * LINKS2 + FRONT)
                select(k)
                if not last:
                    norms(k + 1)
                    assert link.n == LINKS2, link.n
                add_shared(k)

            link.start(0)
            norms(0)
            assert link.n == FRONT, link.n
            one_pass(0)
            with dve.Fori(1, NT - 1) as k:
                one_pass(k)
            one_pass(NT - 1, last=True)

            link.start(NT * LINKS2)
            count = base[:, 0, :]
            link.done(nc.vector.tensor_scalar(nblk[:], count, 1.0 / P, (P - 1) / (2.0 * P), ALU.mult, ALU.add)).wait()
            link.done(nc.vector.tensor_copy(nblk_i[:], nblk[:])).wait()
            link.done(nc.vector.tensor_copy(nblk[:], nblk_i[:])).wait()
            link.done(nc.vector.tensor_tensor_scan(cum[:], ones[:, 0:E], nblk[:], 0.0, ALU.mult, ALU.add)).wait()
            i_e = blk_no[:].unsqueeze(2).broadcast_to([1, NBLK, E])
            link.done(nc.vector.tensor_tensor(passed[:, 0], i_e, cum[0:1].unsqueeze(1).broadcast_to([1, NBLK, E]),
                                              ALU.is_ge)).wait()
            link.done(nc.vector.tensor_tensor(passed[:, 1], passed[:, 0],
                                              nblk[0:1].unsqueeze(1).broadcast_to([1, NBLK, E]), ALU.mult)).wait()
            link.done(nc.vector.tensor_reduce(bexp[:, 0:2, :], passed[:], AX_X, ALU.add)).wait()
            link.done(nc.vector.tensor_tensor(bexp[:, 1, :], blk_no[:], bexp[:, 1, :], ALU.subtract)).wait()
            link.done(nc.vector.tensor_scalar(bexp[:, 1, :], bexp[:, 1, :], float(P), None, ALU.mult)).wait()
            link.done(nc.vector.scalar_tensor_tensor(out=bexp[:, 2, :], in0=bexp[:, 0, :], scalar=float(REGION),
                                                     in1=bexp[:, 1, :], op0=ALU.mult, op1=ALU.add))
            link.done(nc.vector.tensor_tensor(row1[:], count[0:1], region[0:1, :], ALU.add)).wait()
            link.done(nc.vector.tensor_tensor(shift[:, 0, :], cum[:], nblk[:], ALU.subtract)).wait()
            link.done(nc.vector.scalar_tensor_tensor(out=shift[:, 1, :], in0=shift[:, 0, :], scalar=float(P),
                                                     in1=region[:], op0=ALU.mult, op1=ALU.subtract)).wait()
            link.done(nc.vector.tensor_copy(shift[:, 2, :], shift[:, 1, :])).wait()
            link.done(nc.vector.tensor_tensor(shift[:, 2, 1:E], shift[:, 1, 1:E], shift[:, 1, 0:E - 1],
                                              ALU.subtract)).wait()
            many = [P, TOPK * NSUBS, E]
            past = nT[:].rearrange("p c t -> p (c t)")[:, 0:TOPK * NSUBS * E].rearrange("p (n e) -> p n e", e=E)
            flat = rows_of[:].rearrange("p j t -> p (j t)")
            link.done(nc.vector.tensor_tensor(past, flat.unsqueeze(2).broadcast_to(many),
                                              region[:].unsqueeze(1).broadcast_to(many), ALU.is_ge)).wait()
            link.done(nc.vector.tensor_tensor(past, past, shift[:, 2:3, :].broadcast_to(many), ALU.mult)).wait()
            link.done(nc.vector.tensor_reduce(shifts[:], past, AX_X, ALU.add)).wait()
            link.done(nc.vector.tensor_tensor(slots[:].rearrange("p j t -> p (j t)"), flat, shifts[:], ALU.add))
            link.done(nc.vector.tensor_copy(block_row[:], bexp[:, 2, :]))
            link.done(nc.vector.tensor_copy(tail_row[:], row1[:])).wait()
            nc.vector.tensor_scalar(block_exp[:], bexp[:, 0, :], float(E - 1), None, ALU.min).then_inc(table_ready, 1)
            dve.wait_ge(table_ready, 1)

            dve.wait_ge(s_eb2, 16)

            def copy_h(i, par):
                dve.wait_ge(A_done, i + 1)
                nc.vector.tensor_copy(hs[:, par, :].rearrange("p (a n) -> p a n", a=2), psA[:]).then_inc(hs_ready, 1)

            def add_b1(i, par, e):
                dve.wait_ge(HT_done, i + 1)
                bias = vecs[:, ds(e * HC + vec_at["eb1"], HC)].unsqueeze(2).broadcast_to([P, HC, P])
                nc.vector.tensor_tensor(hT[:, par], psY[:, 0:2, :].rearrange("p a (c t) -> p (a c) t", t=P), bias,
                                        ALU.add).then_inc(hb_ready, 1)

            def add_b2(i, par, turn, e):
                dve.wait_ge(B_done, i + 1)
                after(dve, eo_out[par], turn * 16)
                nc.vector.tensor_tensor(eo[:, par, :], psP[:, 1, 0:O], eb2_s[:, e, :], ALU.add).then_inc(eo_ready, 1)

            def block3(i, par, turn, last=False):
                e = dve.value_load(block_exp[0:1, ds(i, 1)], min_val=0, max_val=E - 1)
                add_b1(i, par, e)
                if not last:
                    copy_h(i + 1, 1 - par)
                add_b2(i, par, turn, e)

            copy_h(0, 0)
            def one_pass(t):
                for par in range(2):
                    block3(t * 2 + par, par, t)

            one_pass(0)
            with dve.Fori(1, NBLK // 2 - 1) as t:
                one_pass(t)
            for par in range(2):
                block3(NBLK - 2 + par, par, NBLK // 2 - 1, last=(par == 1))

            stage3_over(dve)

            def hand_slots(b, half):
                nc.vector.tensor_copy(slots4[:, half], slots[:, :, ds(b * (HALVES * NSUB) + half * NSUB, NSUB)]).then_inc(
                    slots4_ready, 1)

            def tile4(b, half):
                t0 = b * (HALVES * NSUB) + half * NSUB
                dve.wait_ge(gathered[half], b * (16 * TOPK * NSUB) + 16 * TOPK * NSUB)
                for j in range(TOPK):
                    for s in range(NSUB):
                        link4.done(nc.vector.scalar_tensor_tensor(
                            out=xall[:, t0 + s, :], in0=gat[:, half, s, j, :], scalar=wts[:, j, ds(t0 + s, 1)],
                            in1=xall[:, t0 + s, :], op0=ALU.mult, op1=ALU.add))
                    link4.wait()
                settled(dve)
                for s in range(NSUB):
                    link4.done(nc.vector.bn_stats(out=st6f[:, half, s, :], in_=xall[:, t0 + s, :]))
                link4.wait()
                settled(dve)
                for s in range(NSUB):
                    link4.done(nc.vector.bn_aggr(out=mvf[:, half, s, :], in_=st6f[:, half, s, :]))
                link4.wait()
                nc.vector.tensor_scalar(scf[:, half, 0, :], mvf[:, half, :, 1], 1e-5, None, ALU.add).then_inc(v4_ready, 1)
                dve.wait_ge(sq4_ready, b * HALVES + (half + 1))
                link4.done(nc.vector.reciprocal(scf[:, half, 1, :], scf[:, half, 1, :])).wait()
                after(dve, out_done[half], b * 16)
                for s in range(NSUB):
                    ins = nc.vector.tensor_scalar(fin[:, half, s, :], xall[:, t0 + s, :], mvf[:, half, s, 0:1],
                                                  scf[:, half, 1, s:s + 1], ALU.subtract, ALU.mult)
                ins.then_inc(fin_ready, 1)

            link4 = Chain(dve, f_link)
            for half in range(HALVES):
                hand_slots(0, half)
            def one_pass(b):
                link4.start(b * (HALVES * LINKS4))
                for half in range(HALVES):
                    tile4(b, half)
                    hand_slots(b + 1, half)
                assert link4.n == HALVES * LINKS4, link4.n

            one_pass(0)
            with dve.Fori(1, NB - 1) as b:
                one_pass(b)
            link4.start((NB - 1) * (HALVES * LINKS4))
            for half in range(HALVES):
                tile4(NB - 1, half)

        @block.tensor
        def _(pe):
            pe.wait_ge(s_const, 5)
            pe.wait_ge(s_w1, W1_DMAS * 16)
            nc.tensor.transpose(psP[0:P, 0, 0:NV], vrows[0:NV, :], ident[0:NV, 0:NV]).then_inc(s_vecT, 1)
            pe.wait_ge(s_setup, SETUP)

            def fill(b, half, use):
                i = bank_of(b, half, use)
                after(pe, p_free[i], uses_before(b, half, use))
                return psP[:, i, :]

            def transposes(b, half, d):
                pe.wait_ge(xr_ready, tile_count(b, half, 1, 1))
                dst = fill(b, half, ("T", d))
                for s in range(NSUB):
                    ins = nc.tensor.transpose(dst[:, s * P:(s + 1) * P], xr[:, s, d * P:(d + 1) * P], ident[:])
                ins.then_inc(p_full, 1)

            def in_proj(b, half, m):
                dst = fill(b, half, ("I", m))
                if m == 0:
                    evacuated(pe, b, half, ("T", 0), ("T", 1))
                for d in range(DC):
                    ins = nc.tensor.matmul(dst, w_in_s[:, d, m * P:(m + 1) * P], xnT[:, d, :],
                                           start=(d == 0), stop=(d == DC - 1))
                ins.then_inc(p_full, 1)

            def conv(b, half, c):
                dst = fill(b, half, ("C", c))
                if c == 0:
                    evacuated(pe, b, half, ("I", CH - 2), ("I", CH - 1))
                    pe.wait_ge(halo_ready, tile_count(b, half, 1, 1))
                for j in range(K):
                    ins = nc.tensor.matmul(dst, convd[:, j * CH + c, :], xraw[:, c, j:j + TC],
                                           start=(j == 0), stop=(j == K - 1))
                ins.then_inc(p_full, 1)

            def x_proj(b, half):
                dst = fill(b, half, ("X", 0))
                pe.wait_ge(xs_ready, tile_count(b, half, 1, 1))
                for c in range(CH):
                    ins = nc.tensor.matmul(dst[0:R + 2 * N, :], w_xp_s[:, c, :], xs[:, c, :],
                                           start=(c == 0), stop=(c == CH - 1))
                ins.then_inc(p_full, 1)

            def dt_proj(b, half, c):
                dst = fill(b, half, ("D", c))
                if c == 0:
                    evacuated(pe, b, half, ("X", 0))
                nc.tensor.matmul(dst, w_dt_s[:, c * P:(c + 1) * P], proj[0:R, :],
                                 start=True, stop=True).then_inc(p_full, 1)

            PE_PARTS = {0: [(transposes, 0), (transposes, 1)], 1: [(in_proj, 0), (in_proj, 1)],
                        2: [(in_proj, 2), (in_proj, 3)], 3: [(conv, 0)], 4: [(conv, 1)], 5: [(conv, 2)],
                        6: [(conv, 3)], 7: [(in_proj, 4)], 8: [(x_proj,)], 9: [(dt_proj, 0), (dt_proj, 1)],
                        10: [(dt_proj, 2), (dt_proj, 3)], 11: [(in_proj, 5)], 12: [(in_proj, 6)],
                        13: [(in_proj, 7)]}

            def prep_part(n, b, half):
                for part, *which in PE_PARTS.get(n, ()):
                    part(b, half, *which)

            def skip(b, half):
                after(pe, z_done, tile_count(b, half, 1, 0))
                for c in range(CH):
                    nc.tensor.matmul(psY[:, c, :], skipd[:, c, :], xs[:, c, :], start=True, stop=False)

            def add_state(b, half, n):
                pe.wait_ge(hc_ready, tile_count(b, half, N, n + 1))
                for c in range(CH):
                    ins = nc.tensor.matmul(psY[:, c, :], ident[:], X[:, n % NX, c, :],
                                           start=False, stop=(n == N - 1))
                ins.then_inc(y_acc, 1)

            def out_proj(b, half):
                pe.wait_ge(z_done, tile_count(b, half, 1, 1))
                for j in range(2):
                    dst = fill(b, half, ("O", j))
                    for i in range(2):
                        s = 2 * j + i
                        for c in range(CH):
                            ins = nc.tensor.matmul(dst[:, i * D:(i + 1) * D], res[:, half, c, s * P:(s + 1) * P],
                                                   w_out_s[:, c, :], start=(c == 0), stop=(c == CH - 1))
                    ins.then_inc(p_full, 1)

            def period(b, half, first=False, last=False):
                skip(b, half)
                if not first:
                    out_proj(*previous(b, half))
                for n in range(N):
                    if not last:
                        prep_part(n, *following(b, half))
                    add_state(b, half, n)

            for n in sorted(PE_PARTS):
                prep_part(n, 0, 0)
            period(0, 0, first=True)
            period(0, 1)
            with pe.Fori(1, NB - 1) as b:
                for half in range(HALVES):
                    period(b, half)
            period(NB - 1, 0)
            period(NB - 1, 1, last=True)
            out_proj(NB - 1, 1)

            stage1_over(pe)
            pe.wait_ge(s_w2, 4 * 16)
            for d in range(DC):
                ins = nc.tensor.transpose(psA[:, 0, d * E:(d + 1) * E], rw[:, d * P:(d + 1) * P], ident[0:E, 0:E])
            ins.then_inc(rwT_full, 1)
            pe.wait_ge(rwT_ready, 1)

            def up(k, m):
                after(pe, relu_done, k * HC + max(m - 1, 0))
                for d in range(DC):
                    ins = nc.tensor.matmul(psP[:, m % 2, :], sw1_s[:, d, m * P:(m + 1) * P], nT[:, d, :],
                                           start=(d == 0), stop=(d == DC - 1))
                ins.then_inc(h_full, 1)

            def down(k, m):
                pe.wait_ge(relu_done, k * HC + (m + 1))
                if m == 0:
                    after(pe, acc_done, k)
                for s in range(NSUB):
                    ins = nc.tensor.matmul(psY[:, s, 0:O], hT2[:, m % NH, s * P:(s + 1) * P], sw2_s[:, m, :],
                                           start=(m == 0), stop=(m == HC - 1))
                ins.then_inc(o_done, 1)

            def positions(k):
                pe.wait_ge(sel_ready, k + 1)
                sel = top[:, TOPK].rearrange("p s e -> p (s e)")
                nc.tensor.matmul(psA[:, 1, 0:NSUB * E], tri[:], sel, start=True, stop=True)
                nc.tensor.matmul(psA[:, 1, NSUB * E:2 * NSUB * E], ones[:], sel, start=True, stop=True).then_inc(
                    pos_full, 1)

            def rows_up(k):
                pe.wait_ge(nrm_ready, k + 1)
                after(pe, slots_ready, k)
                for d in range(DC):
                    for s in range(NSUB):
                        ins = nc.tensor.transpose(psA[:, d, s * P:(s + 1) * P], nrm[:, s, d * P:(d + 1) * P], ident[:])
                    ins.then_inc(tr_full, 1)

            def router(k):
                pe.wait_ge(nT_ready, k * DC + DC)
                for s in range(NSUB):
                    for d in range(DC):
                        ins = nc.tensor.matmul(psA[:, 0, s * E:(s + 1) * E], nT[:, d, s * P:(s + 1) * P], rwT[:, d, :],
                                               start=(d == 0), stop=(d == DC - 1))
                ins.then_inc(logit_full, 1)

            def one_pass(k, last=False):
                for m in range(HC):
                    up(k, m)
                    if m == 2:
                        positions(k)
                    if m:
                        down(k, m - 1)
                if not last:
                    rows_up(k + 1)
                down(k, HC - 1)
                if not last:
                    router(k + 1)

            rows_up(0)
            router(0)
            one_pass(0)
            with pe.Fori(1, NT - 1) as k:
                one_pass(k)
            one_pass(NT - 1, last=True)

            pe.wait_ge(table_ready, 1)
            pe.wait_ge(s_w3, 2 * E * 16)

            def rows_T(i, par, turn):
                pe.wait_ge(xb_here[par], turn * 16 + 16)
                after(pe, nTb_ready, i)
                for d in range(DC):
                    ins = nc.tensor.transpose(psP[:, 0, d * P:(d + 1) * P], xb[:, par, d * P:(d + 1) * P], ident[:])
                ins.then_inc(T_done, 1)

            def expert_up(i, par):
                e = pe.value_load(block_exp[0:1, ds(i, 1)], min_val=0, max_val=E - 1)
                pe.wait_ge(nTb_ready, i + 1)
                after(pe, hs_ready, i)
                for a in range(2):
                    for d in range(DC):
                        ins = nc.tensor.matmul(psA[:, a, :], nTb[:, par, d, :], ew1_s[:, e, d, a * TC:(a + 1) * TC],
                                               start=(d == 0), stop=(d == DC - 1))
                ins.then_inc(A_done, 1)

            def hidden_T(i, par):
                pe.wait_ge(hs_ready, i + 1)
                after(pe, hb_ready, i)
                for m in range(HC):
                    ins = nc.tensor.transpose(psY[:, m // 4, (m % 4) * P:(m % 4 + 1) * P],
                                              hs[:, par, m * P:(m + 1) * P], ident[:])
                ins.then_inc(HT_done, 1)

            def expert_down(i, par):
                e = pe.value_load(block_exp[0:1, ds(i, 1)], min_val=0, max_val=E - 1)
                pe.wait_ge(hr_ready, i + 1)
                after(pe, eo_ready, i)
                for m in range(HC):
                    ins = nc.tensor.matmul(psP[:, 1, 0:O], hT[:, par, m, :], ew2_s[:, e, m, :],
                                           start=(m == 0), stop=(m == HC - 1))
                ins.then_inc(B_done, 1)

            rows_T(0, 0, 0)
            expert_up(0, 0)
            rows_T(1, 1, 0)
            def one_pass(t):
                for par in range(2):
                    i = t * 2 + par
                    hidden_T(i, par)
                    expert_up(i + 1, 1 - par)
                    expert_down(i, par)
                    rows_T(i + 2, par, t + 1)

            one_pass(0)
            with pe.Fori(1, NBLK // 2 - 1) as t:
                one_pass(t)
            hidden_T(NBLK - 2, 0)
            expert_up(NBLK - 1, 1)
            expert_down(NBLK - 2, 0)
            hidden_T(NBLK - 1, 1)
            expert_down(NBLK - 1, 1)


_INS = ['x', 'norm_scale', 'w_in', 'conv_w', 'conv_b', 'A_log', 'D', 'w_xproj', 'w_dt', 'b_dt', 'w_out']
_FFN = ['norm_weight', 'router_w', 'sw1', 'sb1', 'sw2', 'sb2', 'ew1', 'eb1', 'ew2', 'eb2']


def kernel(**inputs):
    import numpy as _np
    import concourse.bacc as _bacc
    from concourse import mybir as _mybir
    from concourse.bass_utils import run_bass_kernel_spmd as _run

    nc = _bacc.Bacc("TRN2", target_bir_lowering=False, num_devices=1)
    arrays, args = {}, []
    for name in ['L0_attn_' + n for n in _INS] + ['L0_ffn_' + n for n in _FFN]:
        a = _np.ascontiguousarray(inputs[name])
        arrays[f"in_{name}_dram"] = a
        args.append(nc.dram_tensor(f"in_{name}_dram", a.shape, _mybir.dt.from_np(a.dtype), kind="ExternalInput").ap())
    shape = inputs['L0_attn_x'].shape
    args.append(nc.dram_tensor("out_0_dram", shape, _mybir.dt.float32, kind="ExternalOutput").ap())
    build(nc, *args)
    r = _run(nc, [arrays], core_ids=[0])
    return r.results[0]["out_0_dram"]
```
